# Optimizing a Trainium2 kernel written in Bass

```python
import numpy as np
import jax
import jax.numpy as jnp

def _softmax(x, axis=-1):
    return jax.nn.softmax(x, axis=axis)

def _gelu(x):
    return jax.nn.gelu(x, approximate=True)

def _silu(x):
    return jax.nn.silu(x)

def _sigmoid(x):
    return jax.nn.sigmoid(x)

def _layernorm(x, axis=-1, eps=1e-05):
    m = jnp.mean(x, axis=axis, keepdims=True)
    v = jnp.var(x, axis=axis, keepdims=True)
    return (x - m) / jnp.sqrt(v + eps)

def _scatter_add(tgt, idx, src, axis=0):
    return tgt.at[idx].add(src)

def _segment_sum(src, seg, n):
    return jax.ops.segment_sum(src, seg, n)
kernel_name = 'mk_gnn_preln_d4_gnn_r8_822c39'

def setup_inputs(seed: int=0):
    np.random.seed(seed)
    _w = jnp.asarray

    def _rec_inputs():
        import jax
        import jax.numpy as jnp
        _gk = jax.random.key(seed)
        x = -0.0001978 + 0.9998 * jax.random.normal(jax.random.fold_in(_gk, 1), (12500, 128), jnp.float32)
        _s = jax.random.randint(jax.random.fold_in(_gk, 2), (100000,), 0, 12500, jnp.int32)
        _d = jax.random.randint(jax.random.fold_in(_gk, 3), (100000,), 0, 12500, jnp.int32)
        _loop = jnp.arange(12500, dtype=jnp.int32)
        src = jnp.concatenate([_s, _d, _loop])
        dst = jnp.concatenate([_d, _s, _loop])
        _o = jnp.argsort(dst, stable=True)
        src = src[_o]
        dst = dst[_o]
        edge_attr_256 = 1.29448e-05 + 0.99998 * jax.random.normal(jax.random.fold_in(_gk, 11), (212500, 256), jnp.float32)
        edge_type_4 = jax.random.randint(jax.random.fold_in(_gk, 14), (212500,), 0, 4, jnp.int32)
        edge_weight = -0.000492943 + 0.999642 * jax.random.normal(jax.random.fold_in(_gk, 15), (212500,), jnp.float32)
        return (x, src, dst, edge_attr_256, edge_type_4, edge_weight)
    x, src, dst, edge_attr_256, edge_type_4, edge_weight = _rec_inputs()

    def _L0_gnn_setup():
        import jax, jax.numpy as jnp
        import numpy as np
        N_NODES = 6250
        key = jax.random.key(seed)
        k1, k2, k3 = jax.random.split(key, 3)
        n_edges, num_heads, feat_dim = (125000, 2, 128)
        nbrs = jax.random.randint(k1, (n_edges, 2), 0, N_NODES, dtype=jnp.int64)
        x_i = jax.random.normal(k2, (N_NODES, feat_dim), dtype=jnp.float32)
        scaled_v = jax.random.normal(k3, (n_edges, num_heads * feat_dim), dtype=jnp.float32)
        W = jax.random.normal(jax.random.fold_in(key, 10), (feat_dim, num_heads * feat_dim), dtype=jnp.float32) * (1.0 / np.sqrt(num_heads * feat_dim))
        b = jnp.zeros((feat_dim,), dtype=jnp.float32)
        return {'nbrs': nbrs, 'x_i': x_i, 'scaled_v': scaled_v, 'W': W, 'b': b}
    _L0_gnn_all = _L0_gnn_setup()
    _L0_gnn_in = {k: v for k, v in _L0_gnn_all.items() if k in ('W', 'b')}
    del _L0_gnn_all

    def _L1_gnn_setup():
        import jax, jax.numpy as jnp
        import numpy as np
        N_NODES = 6250
        N_EDGES = 80000
        D_FEAT = 128
        key = jax.random.key(seed)
        kx, ke = jax.random.split(key)
        x = jax.random.normal(kx, (N_NODES, D_FEAT), dtype=jnp.float32)
        edge_index = jax.random.randint(ke, (2, N_EDGES), 0, N_NODES, dtype=jnp.int64)
        return {'x': x, 'edge_index': edge_index}
    _L1_gnn_all = _L1_gnn_setup()
    _L1_gnn_in = {k: v for k, v in _L1_gnn_all.items() if k in ()}
    del _L1_gnn_all

    def _L2_gnn_setup():
        import jax, jax.numpy as jnp
        import numpy as np
        EPS = 1e-09
        LN_EPS = 1e-05

        def _proj_normalize(v):
            return v / (jnp.linalg.norm(v, axis=-1, keepdims=True) + EPS)
        N, E, Fin, Fout = (6250, 75000, 128, 128)
        key = jax.random.key(seed)
        ks = jax.random.split(key, 8)
        x = jax.random.normal(ks[0], (N, Fin), jnp.float32)
        edge_index = jax.random.randint(ks[1], (2, E), 0, N, dtype=jnp.int64)
        edge_weight = jax.random.normal(ks[2], (E,), jnp.float32)
        W_self = jax.random.normal(ks[3], (Fin, Fout), jnp.float32) / np.sqrt(Fin)
        b_self = jnp.zeros((Fout,), jnp.float32)
        W_nb = jax.random.normal(ks[4], (Fin, Fout), jnp.float32) / np.sqrt(Fin)
        b_nb = jnp.zeros((Fout,), jnp.float32)
        gamma = jnp.ones((Fout,), jnp.float32)
        beta = jnp.zeros((Fout,), jnp.float32)
        return dict(x=x, edge_index=edge_index, edge_weight=edge_weight, W_self=W_self, b_self=b_self, W_nb=W_nb, b_nb=b_nb, gamma=gamma, beta=beta)
    _L2_gnn_all = _L2_gnn_setup()
    _L2_gnn_in = {k: v for k, v in _L2_gnn_all.items() if k in ('W_self', 'b_self', 'W_nb', 'b_nb', 'gamma', 'beta')}
    del _L2_gnn_all

    def _L3_gnn_setup():
        import jax, jax.numpy as jnp
        import numpy as np
        N_NODES = 12500
        N_EDGES = 75000
        N_REL = 4
        N_HEADS = 4
        DIM = 128
        HEAD_DIM = DIM // N_HEADS
        NEG_SLOPE = 0.2
        key = jax.random.key(seed)
        k1, k2, k3, k4, k5 = jax.random.split(key, 5)
        x = jax.random.normal(k1, (N_NODES, DIM), dtype=jnp.float32)
        edge_index = jax.random.randint(k2, (2, N_EDGES), 0, N_NODES, dtype=jnp.int64)
        edge_types = jax.random.randint(k3, (N_EDGES,), 0, N_REL, dtype=jnp.int64)
        W = jax.random.normal(k4, (N_REL, DIM, DIM), dtype=jnp.float32) * (1.0 / np.sqrt(DIM))
        attn = jax.random.normal(k5, (N_REL, N_HEADS, 2 * HEAD_DIM), dtype=jnp.float32) * 0.1
        return {'x': x, 'edge_index': edge_index, 'edge_types': edge_types, 'W': W, 'attn': attn}
    _L3_gnn_all = _L3_gnn_setup()
    _L3_gnn_in = {k: v for k, v in _L3_gnn_all.items() if k in ('W', 'attn')}
    del _L3_gnn_all
    return {'x': x, 'src': src, 'dst': dst, 'edge_attr_256': edge_attr_256, 'edge_type_4': edge_type_4, 'edge_weight': edge_weight, 'L0_gnn_W': _L0_gnn_in['W'], 'L0_gnn_b': _L0_gnn_in['b'], 'L2_gnn_W_self': _L2_gnn_in['W_self'], 'L2_gnn_b_self': _L2_gnn_in['b_self'], 'L2_gnn_W_nb': _L2_gnn_in['W_nb'], 'L2_gnn_b_nb': _L2_gnn_in['b_nb'], 'L2_gnn_gamma': _L2_gnn_in['gamma'], 'L2_gnn_beta': _L2_gnn_in['beta'], 'L3_gnn_W': _L3_gnn_in['W'], 'L3_gnn_attn': _L3_gnn_in['attn']}

def reference(x, src, dst, edge_attr_256, edge_type_4, edge_weight, L0_gnn_W, L0_gnn_b, L2_gnn_W_self, L2_gnn_b_self, L2_gnn_W_nb, L2_gnn_b_nb, L2_gnn_gamma, L2_gnn_beta, L3_gnn_W, L3_gnn_attn):
    import jax
    import jax.numpy as jnp

    def _L0_gnn_ref(nbrs, x_i, scaled_v, W, b):
        import jax, jax.numpy as jnp
        import numpy as np
        N_NODES = 6250
        x_i_prime = jax.ops.segment_sum(scaled_v, nbrs[:, 0], num_segments=x_i.shape[0])
        return x_i + x_i_prime @ W.T + b

    def _L1_gnn_ref(x, edge_index):
        import jax, jax.numpy as jnp
        import numpy as np
        N_NODES = 6250
        N_EDGES = 80000
        D_FEAT = 128
        row, col = (edge_index[0], edge_index[1])
        n = x.shape[0]
        ones = jnp.ones(row.shape[0], dtype=x.dtype)
        deg = jax.ops.segment_sum(ones, col, num_segments=n)
        deg_inv_sqrt = jnp.where(deg > 0, jax.lax.rsqrt(jnp.maximum(deg, 1.0)), 0.0)
        norm = deg_inv_sqrt[row] * deg_inv_sqrt[col]
        msg = x[row] * norm[:, None]
        out = jax.ops.segment_sum(msg, col, num_segments=n)
        return out

    def _L2_gnn_ref(x, edge_index, edge_weight, W_self, b_self, W_nb, b_nb, gamma, beta):
        import jax, jax.numpy as jnp
        import numpy as np
        EPS = 1e-09
        LN_EPS = 1e-05

        def _proj_normalize(v):
            return v / (jnp.linalg.norm(v, axis=-1, keepdims=True) + EPS)
        N = x.shape[0]
        src, tgt = (edge_index[0], edge_index[1])
        seg_max = jax.ops.segment_max(edge_weight, tgt, num_segments=N)
        ew = jnp.exp(edge_weight - seg_max[tgt])
        denom = jax.ops.segment_sum(ew, tgt, num_segments=N)
        alpha = ew / denom[tgt]
        agg = jax.ops.segment_sum(alpha[:, None] * x[src], tgt, num_segments=N)
        agg = _proj_normalize(agg)
        self_feat = x @ W_self + b_self
        nb_feat = agg @ W_nb + b_nb
        comb = _proj_normalize(0.5 * (self_feat + nb_feat))
        mu = jnp.mean(comb, axis=-1, keepdims=True)
        var = jnp.var(comb, axis=-1, keepdims=True)
        out = (comb - mu) / jnp.sqrt(var + LN_EPS) * gamma + beta
        return out

    def _L3_gnn_ref(x, edge_index, edge_types, W, attn):
        import jax, jax.numpy as jnp
        import numpy as np
        N_NODES = 12500
        N_EDGES = 75000
        N_REL = 4
        N_HEADS = 4
        DIM = 128
        HEAD_DIM = DIM // N_HEADS
        NEG_SLOPE = 0.2
        N = x.shape[0]
        R, H, twoD = attn.shape
        D = twoD // 2
        E = edge_types.shape[0]
        x_rel = jnp.einsum('ni,rio->rno', x, W).reshape(R, N, H, D)
        src, dst = (edge_index[0], edge_index[1])
        src_feat = x_rel[edge_types, src]
        dst_feat = x_rel[edge_types, dst]
        a = attn[edge_types]
        cat = jnp.concatenate([src_feat, dst_feat], axis=-1)
        alpha = jnp.sum(cat * a, axis=-1)
        alpha = jnp.where(alpha > 0, alpha, NEG_SLOPE * alpha)
        seg = edge_types * N + dst
        S = R * N
        m = jax.ops.segment_max(alpha, seg, num_segments=S)
        alpha_exp = jnp.exp(alpha - m[seg])
        denom = jax.ops.segment_sum(alpha_exp, seg, num_segments=S)
        w = alpha_exp / denom[seg]
        msg = (src_feat * w[..., None]).reshape(E, H * D)
        out = jax.ops.segment_sum(msg, dst, num_segments=N)
        return out
    edge_index = jnp.stack([src, dst])
    edge_index_t = jnp.stack([src, dst], axis=1)
    h = jnp.maximum(_layernorm(x, axis=-1), 0.0)
    x = x + _L0_gnn_ref(edge_index_t, h, edge_attr_256, L0_gnn_W, L0_gnn_b)
    h = jnp.maximum(_layernorm(x, axis=-1), 0.0)
    x = x + _L1_gnn_ref(h, edge_index)
    h = jnp.maximum(_layernorm(x, axis=-1), 0.0)
    x = x + _L2_gnn_ref(h, edge_index, edge_weight, L2_gnn_W_self, L2_gnn_b_self, L2_gnn_W_nb, L2_gnn_b_nb, L2_gnn_gamma, L2_gnn_beta)
    h = jnp.maximum(_layernorm(x, axis=-1), 0.0)
    x = x + _L3_gnn_ref(h, edge_index, edge_type_4, L3_gnn_W, L3_gnn_attn)
    return x

_drawn_inputs = setup_inputs


def setup_inputs(seed=0):
    import zlib

    import numpy as np

    out = dict(_drawn_inputs(seed))
    spreads = {'L0_gnn_b': (0.0, 0.315),
     'L2_gnn_b_self': (0.0, 0.272),
     'L2_gnn_b_nb': (0.0, 0.1),
     'L2_gnn_gamma': (1.0, 0.2),
     'L2_gnn_beta': (0.0, 0.361)}
    factors = {'edge_weight': 6.288}
    for name, (base, spread) in spreads.items():
        noise = np.random.default_rng([zlib.crc32(name.encode()), seed]).standard_normal(out[name].shape)
        drawn = base * np.exp(spread * noise) if base else spread * noise
        out[name] = jnp.asarray(drawn.astype(out[name].dtype))
    for name, factor in factors.items():
        out[name] = (out[name] * factor).astype(out[name].dtype)
    return out
```

```python
from contextlib import ExitStack

import concourse.bass as bass
from concourse import mybir

P = 128
D = 128
DE = 256
R = 4
H = 4
HD = D // H
RH = R * H
XW = D + H
G = 10
K = 5
B = 8
BIG = 1.0e38
LN_EPS = 1e-5
NORM_EPS = 1e-9
SLOPE = 0.2


def steps_per_partition(n_edges):
    return -(-n_edges // (P * 4 * B)) * 4 * B


def node_columns(n_nodes):
    return -(-n_nodes // P)


def chunk_columns(cols):
    return max(c for c in range(1, 9) if cols % (2 * c) == 0)


class Serial:

    def __init__(self, engine, sem):
        self.engine, self.sem, self.base, self.n = engine, sem, 0, 0

    def __call__(self, instruction):
        self.n += 1
        instruction.then_inc(self.sem, 1)
        self.engine.wait_ge(self.sem, self.base + self.n)

    def enter(self, i, per_turn):
        self.start, self.per_turn = self.base + self.n, per_turn
        self.base, self.n = self.start + i * per_turn, 0

    def leave(self, turns):
        assert self.n == self.per_turn, (self.n, self.per_turn)
        self.base, self.n = self.start + turns * self.per_turn, 0


def build_gnn(nc, x_in, src_in, dst_in, type_in, ew_in, tile_src, tile_src_cols, edge_attr,
              w0_in, b0_in, wself_in, wnb_in, bself_in, bnb_in, gamma_in, beta_in, w3_in, attn_in, out):
    f32, i32, bf16 = mybir.dt.float32, mybir.dt.int32, mybir.dt.bfloat16
    ALU = mybir.AluOpType
    ACT = mybir.ActivationFunctionType
    X_AXIS = mybir.AxisListType.X

    J = x_in.shape[1] // D
    NP = P * J
    T = src_in.shape[1]
    EP = P * T
    E = edge_attr.shape[0]
    N = out.shape[0]
    JC = chunk_columns(J)
    NC = J // JC
    PAIRS = E // (2 * G * P)
    U = 2 * PAIRS
    LEFT = E - U * G * P
    NT = (U + 1) * G
    TABLE_ROWS = NP + P
    TURNS = T // (2 * B)
    assert J <= P and 0 < LEFT <= P and T <= NT

    def dram(name, shape, dt=f32):
        return nc.dram_tensor(name, shape, dt, kind="Internal").ap()

    tables = [dram(f"sum_table{k}", (TABLE_ROWS, D)) for k in range(K)]
    h_table = dram("h_table", (NP, D))
    rel_table = dram("rel_table", (NP * R, XW))
    running = dram("running", (EP + P, D))
    rel_edges = dram("rel_edges", (EP, XW))
    adst_nodes = dram("adst_nodes", (NP, RH))
    adst_edges = dram("adst_edges", (EP + NP, RH))
    hi_line = dram("hi_line", (NT * P,), bf16)
    lo_line = dram("lo_line", (NT * P,), bf16)
    deg_line = dram("deg_line", (NP,))
    cum_line = dram("cum_line", (NP,))

    running_steps = running[0:EP, :].rearrange("(p t) d -> p t d", t=T)
    rel_steps = rel_edges.rearrange("(p t) d -> p t d", t=T)
    adst_steps = adst_edges[0:EP, :].rearrange("(p t) c -> p t c", t=T)
    h_columns = h_table.rearrange("(p j) d -> p j d", j=J)
    rel_columns = rel_table.rearrange("(p j r) d -> p j r d", j=J, r=R)
    adst_columns = adst_nodes.rearrange("(p j) c -> p j c", j=J)
    line = bass.ds

    def after(v):
        return v + 3

    ctx = ExitStack()
    with ctx:
        def sem(name):
            return ctx.enter_context(nc.semaphore(name))

        def sb(name, shape, dt=f32, scope=ctx):
            return scope.enter_context(nc.sbuf_tensor(name, shape, dt))

        row_bank = ctx.enter_context(nc.psum_tensor("row_bank", [P, 3 * 512], f32))
        bank = [ctx.enter_context(nc.psum_tensor(f"bank{i}", [P, 512], f32)) for i in range(5)]

        x = sb("x", [P, J * D])
        src_idx = sb("src_idx", [P, T], i32)
        rel_idx = sb("rel_idx", [P, T], i32)
        same = sb("same", [P, T + 1])
        first = sb("first", [P, T], bf16)
        last = sb("last", [P, T], bf16)
        is_type = sb("is_type", [P, R, T], bf16)
        ident = sb("ident", [P, P])
        ones = sb("ones", [P, P])
        row_iota = sb("row_iota", [P, P])
        col_iota = sb("col_iota", [P, 1])
        lower = sb("lower", [P, P])
        upper = sb("upper", [P, P])
        from_before = sb("from_before", [P, P])
        from_after = sb("from_after", [P, P])
        bias_before = sb("bias_before", [P, P])
        bias_after = sb("bias_after", [P, P])
        first_end = sb("first_end", [P, 1], i32)
        first_node = sb("first_node", [P, 1], i32)
        ew_prob = sb("ew_prob", [P, T])
        deg = sb("deg", [P, J])
        dinv = sb("dinv", [P, J])
        node_row = sb("node_row", [P, J], i32)
        node_start = sb("node_start", [P, J], i32)
        w0t = sb("w0t", [P, 2, D])
        wself = sb("wself", [P, D])
        wnb = sb("wnb", [P, D])
        gamma = sb("gamma", [P, D])
        beta = sb("beta", [P, D])
        half_bias = sb("half_bias", [P, D])
        w3 = sb("w3", [P, R * D])
        w3_score = sb("w3_score", [P, 2 * RH])
        hist = sb("hist", [P, P])
        passed = sem("passed")
        added = [sem(f"added{k}") for k in range(K)]
        zeros_out = sem("zeros_out")
        dve_own = sem("dve_own")
        own_count = [0]

        class Vector(Serial):

            def __init__(self, engine):
                Serial.__init__(self, engine, dve_own)
                self.base = own_count[0]

            def close(self):
                own_count[0] = self.base + self.n

        def columns(c, k):
            return x[:, bass.ds((c * JC + k) * D, D)]

        def chunk(c):
            return x[:, bass.ds(c * JC * D, JC * D)].rearrange("p (j d) -> p j d", d=D)

        class Norm:

            def __init__(self, name, scope):
                self.stats = sb(f"{name}_stats", [P, JC, 6], f32, scope)
                self.mv = sb(f"{name}_mv", [P, JC, 2], f32, scope)
                self.var = sb(f"{name}_var", [P, JC], f32, scope)
                self.std = sb(f"{name}_std", [P, JC], f32, scope)
                self.scale = sb(f"{name}_scale", [P, JC], f32, scope)
                self.shift = sb(f"{name}_shift", [P, JC], f32, scope)
                self.var_ready = sem(f"{name}_var_ready")
                self.std_ready = sem(f"{name}_std_ready")
                self.shift_ready = sem(f"{name}_shift_ready")
                self.out_ready = sem(f"{name}_out_ready")

            OWN = 3

            def vector(self, dve, own, c, col, factor=None):
                dve.sem_inc(passed, 1)
                for k in range(JC):
                    ins = nc.vector.bn_stats(self.stats[:, k, :], col(k))
                own(ins)
                dve.sem_inc(passed, 1)
                for k in range(JC):
                    ins = nc.vector.bn_aggr(self.mv[:, k, :], self.stats[:, k, :])
                own(ins)
                nc.vector.tensor_scalar(self.var[:, :], self.mv[:, :, 1], LN_EPS, None,
                                        ALU.add).then_inc(self.var_ready, 1)
                dve.wait_ge(self.std_ready, c + 1)
                own(nc.vector.reciprocal(self.scale[:, :], self.std[:, :]))
                if factor is not None:
                    own(nc.vector.tensor_tensor(self.scale[:, :], self.scale[:, :], factor, ALU.mult))
                nc.vector.scalar_tensor_tensor(out=self.shift[:, :], in0=self.mv[:, :, 0], scalar=-1.0,
                                               in1=self.scale[:, :], op0=ALU.mult,
                                               op1=ALU.mult).then_inc(self.shift_ready, 1)

            def scalar_std(self, act, c):
                act.wait_ge(self.var_ready, c + 1)
                nc.scalar.activation(self.std[:, :], self.var[:, :], ACT.Sqrt).then_inc(self.std_ready, 1)

            def scalar_apply(self, act, c, col, to, func):
                act.wait_ge(self.shift_ready, c + 1)
                for k in range(JC):
                    ins = nc.scalar.activation(to(k), col(k), func, bias=self.shift[:, k:k + 1],
                                               scale=self.scale[:, k:k + 1])
                ins.then_inc(self.out_ready, 1)

        with ExitStack() as ph:
            zeros = sb("zeros", [P, TABLE_ROWS // 8], f32, ph)
            dst_i = sb("dst_i", [P, T], i32, ph)
            dstf = sb("dstf", [P, T], f32, ph)
            type_i = sb("type_i", [P, T], i32, ph)
            typef = sb("typef", [P, T], f32, ph)
            srcf = sb("srcf", [P, T], f32, ph)
            ew = sb("ew", [P, T], f32, ph)
            scan_a = sb("scan_a", [P, T], f32, ph)
            scan_b = sb("scan_b", [P, T], f32, ph)
            neg = sb("neg", [P, T + 1], f32, ph)
            w0 = sb("w0", [P, DE], f32, ph)
            b0 = sb("b0", [P, D], f32, ph)
            bself = sb("bself", [P, D], f32, ph)
            bnb = sb("bnb", [P, D], f32, ph)
            attn = sb("attn", [P, 2 * R * D], f32, ph)
            w3a = sb("w3a", [P, R * D], f32, ph)
            diag = sb("diag", [P, 2, P], f32, ph)
            edge_val = sb("edge_val", [P, 8], f32, ph)
            masked = sb("masked", [P, P], f32, ph)
            cnt = sb("cnt", [P, 2], f32, ph)
            h0 = sb("h0", [P, JC, D], f32, ph)
            line_i = sb("line_i", [P, NT], i32, ph)
            line_half = sb("line_half", [P, NT], i32, ph)
            line_bf = sb("line_bf", [P, 2, NT], bf16, ph)

            edges_in = sem("edges_in")
            nodes_in = sem("nodes_in")
            weights_in = sem("weights_in")
            line_in = sem("line_in")
            line_split = sem("line_split")
            lines_out = sem("lines_out")
            iotas = sem("iotas")
            zeros_set = sem("zeros_set")
            diags = sem("diags")
            rows_ready = sem("rows_ready")
            w0_turned = sem("w0_turned")
            max_edges = sem("max_edges")
            max_rows = sem("max_rows")
            ew_shift = sem("ew_shift")
            ew_exp = sem("ew_exp")
            sum_edges = sem("sum_edges")
            sum_carry = sem("sum_carry")
            norm = Norm("norm0", ph)

            block = ph.enter_context(nc.Block("setup"))

            @block.sync
            def _(sp):
                sp.dma_start(dst_i[:, :], dst_in).then_inc(edges_in, 16)
                sp.dma_start(src_idx[:, :], src_in).then_inc(edges_in, 16)
                sp.dma_start(type_i[:, :], type_in).then_inc(edges_in, 16)
                sp.dma_start(ew[:, :], ew_in).then_inc(edges_in, 16)
                sp.dma_start(line_i[:, :], tile_src.rearrange("(p a) -> p a", p=P)).then_inc(line_in, 16)
                sp.dma_start(x[:, :], x_in).then_inc(nodes_in, 16)
                sp.dma_start(b0[:, :], b0_in).then_inc(nodes_in, 16)
                for to, of in ((w0, w0_in), (wself, wself_in), (wnb, wnb_in), (bself, bself_in),
                               (bnb, bnb_in), (gamma, gamma_in), (beta, beta_in), (w3, w3_in),
                               (attn, attn_in)):
                    sp.dma_start(to[:, :], of).then_inc(weights_in, 16)
                sp.wait_ge(line_split, 1)
                sp.dma_start(hi_line.rearrange("(p a) -> p a", p=P), line_bf[:, 0, :]).then_inc(lines_out, 16)
                sp.dma_start(lo_line.rearrange("(p a) -> p a", p=P), line_bf[:, 1, :]).then_inc(lines_out, 16)
                sp.wait_ge(zeros_set, 1)
                width = TABLE_ROWS // 8
                sp.dma_start(running[EP:EP + P, :], zeros[:, 0:D]).then_inc(zeros_out, 16)
                per_row = (EP + NP) * RH // P
                flat = adst_edges.rearrange("(p a) d -> p (a d)", p=P)
                full = per_row // width
                sp.dma_start(flat[:, 0:full * width].rearrange("p (k w) -> p k w", w=width),
                             zeros[:, :].unsqueeze(1).broadcast_to([P, full, width])).then_inc(zeros_out, 16)
                if per_row > full * width:
                    sp.dma_start(flat[:, full * width:per_row],
                                 zeros[:, 0:per_row - full * width]).then_inc(line_in, 16)
                    sp.wait_ge(line_in, 32)
                sp.wait_ge(zeros_out, 32)
                sp.wait_ge(lines_out, 32)

            @block.gpsimd
            def _(pool):
                nc.gpsimd.iota(row_iota[:, :], [[1, P]], base=0, channel_multiplier=0,
                               allow_small_or_imprecise_dtypes=True).then_inc(iotas, 1)
                nc.gpsimd.iota(col_iota[:, :], [[0, 1]], base=0, channel_multiplier=1,
                               allow_small_or_imprecise_dtypes=True).then_inc(iotas, 1)
                nc.gpsimd.memset(zeros[:, :], 0.0).then_inc(zeros_set, 1)
                pool.wait_ge(zeros_set, 1)
                width = TABLE_ROWS // 8
                for k in range(K):
                    nc.gpsimd.dma_start(
                        tables[k].rearrange("(p a) d -> p (a d)", p=P).rearrange("p (k w) -> p k w", w=width),
                        zeros[:, :].unsqueeze(1).broadcast_to([P, 8, width])).then_inc(added[k], 16)
                for k in range(K):
                    pool.wait_ge(added[k], 16)

            @block.vector
            def _(dve):
                own = Vector(dve)
                dve.wait_ge(line_in, 16)
                own(nc.vector.tensor_scalar(line_half[:, :], line_i[:, :], 7, None, ALU.logical_shift_right))
                own(nc.vector.tensor_copy(line_bf[:, 0, :], line_half[:, :]))
                own(nc.vector.tensor_scalar(line_half[:, :], line_i[:, :], 127, None, ALU.bitwise_and))
                nc.vector.tensor_copy(line_bf[:, 1, :], line_half[:, :]).then_inc(line_split, 1)

                dve.wait_ge(iotas, 2)
                nc.vector.tensor_scalar(ident[:, :], row_iota[:, :], col_iota[:, :], None, ALU.is_equal)
                nc.vector.tensor_scalar(lower[:, :], row_iota[:, :], col_iota[:, :], None, ALU.is_lt)
                nc.vector.tensor_scalar(upper[:, :], row_iota[:, :], col_iota[:, :], None, ALU.is_gt)
                nc.vector.memset(ones[:, :], 1.0)
                own(nc.vector.memset(hist[:, :], 0.0))

                dve.wait_ge(edges_in, 64)
                nc.vector.memset(same[:, 0:1], 0.0)
                nc.vector.memset(same[:, T:T + 1], 0.0)
                nc.vector.tensor_copy(first_node[:, :], dst_i[:, 0:1])
                nc.vector.tensor_copy(srcf[:, :], src_idx[:, :])
                nc.vector.tensor_copy(typef[:, :], type_i[:, :])
                own(nc.vector.tensor_copy(dstf[:, :], dst_i[:, :]))
                nc.vector.tensor_tensor(same[:, 1:T], dstf[:, 1:T], dstf[:, 0:T - 1], ALU.is_equal)
                nc.vector.tensor_scalar(first[:, :], dstf[:, :], dstf[:, 0:1], None, ALU.is_equal)
                nc.vector.tensor_scalar(last[:, :], dstf[:, :], dstf[:, T - 1:T], None, ALU.is_equal)
                for r in range(R):
                    nc.vector.tensor_scalar(is_type[:, r, :], typef[:, :], float(r), None, ALU.is_equal)
                nc.vector.scalar_tensor_tensor(out=rel_idx[:, :], in0=srcf[:, :], scalar=float(R),
                                               in1=typef[:, :], op0=ALU.mult, op1=ALU.add)
                nc.vector.tensor_scalar(diag[:, 0, :], ident[:, :], dstf[:, 0:1], None, ALU.mult)
                nc.vector.tensor_scalar(diag[:, 1, :], ident[:, :], dstf[:, T - 1:T], None,
                                        ALU.mult).then_inc(diags, 1)
                dve.wait_ge(diags, 1)
                own(nc.vector.tensor_scalar(neg[:, :], same[:, :], -1.0, BIG, ALU.add, ALU.mult))
                own(nc.vector.reduce_sum(cnt[:, 0:1], first[:, :], X_AXIS))
                own(nc.vector.tensor_scalar(cnt[:, 1:2], col_iota[:, :], float(T), -1.0, ALU.mult, ALU.add))
                own(nc.vector.tensor_tensor(first_end[:, :], cnt[:, 0:1], cnt[:, 1:2], ALU.add))
                dve.wait_ge(rows_ready, 1)
                nc.vector.scalar_tensor_tensor(out=from_before[:, :], in0=bank[0][:, 0:P],
                                               scalar=dstf[:, T - 1:T], in1=upper[:, :],
                                               op0=ALU.is_equal, op1=ALU.mult)
                own(nc.vector.scalar_tensor_tensor(out=from_after[:, :], in0=bank[1][:, 0:P],
                                                   scalar=dstf[:, 0:1], in1=lower[:, :],
                                                   op0=ALU.is_equal, op1=ALU.mult))
                nc.vector.tensor_scalar(bias_before[:, :], from_after[:, :], -1.0, BIG, ALU.add, ALU.mult)
                own(nc.vector.tensor_scalar(bias_after[:, :], from_before[:, :], -1.0, BIG, ALU.add, ALU.mult))

                own(nc.vector.tensor_tensor_scan(scan_a[:, :], neg[:, 0:T], ew[:, :], 0.0, ALU.add, ALU.max))
                own(nc.vector.tensor_tensor_scan(scan_b[:, ::-1], neg[:, 1:T + 1][:, ::-1],
                                                 scan_a[:, ::-1], 0.0, ALU.add, ALU.max))
                nc.vector.tensor_scalar(diag[:, 0, :], ident[:, :], scan_a[:, T - 1:T], None, ALU.mult)
                nc.vector.tensor_scalar(diag[:, 1, :], ident[:, :], scan_b[:, 0:1], None,
                                        ALU.mult).then_inc(max_edges, 1)
                dve.wait_ge(max_rows, 1)
                own(nc.vector.tensor_tensor(masked[:, :], bank[0][:, 0:P], bias_before[:, :], ALU.add))
                own(nc.vector.tensor_reduce(edge_val[:, 0:1], masked[:, :], X_AXIS, ALU.max))
                own(nc.vector.tensor_tensor(masked[:, :], bank[1][:, 0:P], bias_after[:, :], ALU.add))
                own(nc.vector.tensor_reduce(edge_val[:, 1:2], masked[:, :], X_AXIS, ALU.max))
                for mask, k in ((first, 0), (last, 1)):
                    own(nc.vector.tensor_scalar(scan_a[:, :], mask[:, :], -1.0, BIG, ALU.add, ALU.mult))
                    own(nc.vector.scalar_tensor_tensor(out=scan_b[:, :], in0=scan_a[:, :],
                                                       scalar=edge_val[:, k:k + 1], in1=scan_b[:, :],
                                                       op0=ALU.add, op1=ALU.max))
                nc.vector.tensor_tensor(scan_a[:, :], ew[:, :], scan_b[:, :], ALU.subtract).then_inc(ew_shift, 1)
                dve.wait_ge(ew_exp, 1)
                own(nc.vector.tensor_tensor_scan(scan_a[:, :], same[:, 0:T], ew[:, :], 0.0, ALU.mult, ALU.add))
                own(nc.vector.tensor_copy(edge_val[:, 2:3], scan_a[:, T - 1:T]))
                own(nc.vector.scalar_tensor_tensor(out=scan_b[:, :], in0=same[:, 1:T + 1], scalar=1.0,
                                                   in1=scan_a[:, :], op0=ALU.is_lt, op1=ALU.mult))
                own(nc.vector.tensor_tensor_scan(scan_a[:, ::-1], same[:, 1:T + 1][:, ::-1],
                                                 scan_b[:, ::-1], 0.0, ALU.mult, ALU.add))
                nc.vector.tensor_copy(edge_val[:, 3:4], scan_a[:, 0:1]).then_inc(sum_edges, 1)
                dve.wait_ge(sum_carry, 1)
                own(nc.vector.tensor_copy(edge_val[:, 4:6], bank[2][:, 0:2]))
                own(nc.vector.scalar_tensor_tensor(out=scan_b[:, :], in0=first[:, :], scalar=edge_val[:, 4:5],
                                                   in1=scan_a[:, :], op0=ALU.mult, op1=ALU.add))
                own(nc.vector.scalar_tensor_tensor(out=scan_a[:, :], in0=last[:, :], scalar=edge_val[:, 5:6],
                                                   in1=scan_b[:, :], op0=ALU.mult, op1=ALU.add))
                own(nc.vector.reciprocal(scan_b[:, :], scan_a[:, :]))
                own(nc.vector.tensor_tensor(ew_prob[:, :], ew[:, :], scan_b[:, :], ALU.mult))

                dve.wait_ge(weights_in, 16 * 9)
                dve.wait_ge(w0_turned, 1)
                nc.vector.tensor_copy(w0t[:, :, :].rearrange("p c d -> p (c d)"), bank[3][:, 0:2 * D])
                own(nc.vector.tensor_tensor(half_bias[:, :], bself[:, :], bnb[:, :], ALU.add))
                own(nc.vector.tensor_scalar(half_bias[:, :], half_bias[:, :], 0.5, None, ALU.mult))
                for side in range(2):
                    own(nc.vector.tensor_tensor(w3a[:, :], w3[:, :], attn[:, side * R * D:(side + 1) * R * D],
                                                ALU.mult))
                    own(nc.vector.reduce_sum(w3_score[:, side * RH:(side + 1) * RH],
                                             w3a[:, :].rearrange("p (c d) -> p c d", d=HD), X_AXIS))

                dve.wait_ge(nodes_in, 32)
                with dve.Fori(0, NC) as c:
                    own.enter(c, Norm.OWN + 2)
                    norm.vector(dve, own, c, lambda k: columns(c, k))
                    dve.wait_ge(norm.out_ready, c + 1)
                    own(nc.vector.tensor_tensor(chunk(c), chunk(c), h0[:, :, :], ALU.add))
                    own(nc.vector.tensor_tensor(chunk(c), chunk(c),
                                                b0[:, :].unsqueeze(1).broadcast_to([P, JC, D]), ALU.add))
                own.leave(NC)
                own.close()

            @block.scalar
            def _(act):
                act.wait_ge(ew_shift, 1)
                nc.scalar.activation(ew[:, :], scan_a[:, :], ACT.Exp).then_inc(ew_exp, 1)
                act.wait_ge(nodes_in, 32)
                with act.Fori(0, NC) as c:
                    norm.scalar_std(act, c)
                    norm.scalar_apply(act, c, lambda k: columns(c, k), lambda k: h0[:, k, :], ACT.Relu)

            @block.tensor
            def _(pe):
                pe.wait_ge(diags, 1)
                for k in range(2):
                    ins = nc.tensor.matmul(bank[k][:, 0:P], ones[:, :], diag[:, k, :], start=True, stop=True)
                ins.then_inc(rows_ready, 1)
                pe.wait_ge(weights_in, 16 * 9)
                for c in range(2):
                    ins = nc.tensor.transpose(bank[3][:, c * D:(c + 1) * D], w0[:, c * D:(c + 1) * D], ident[:, :])
                ins.then_inc(w0_turned, 1)
                pe.wait_ge(max_edges, 1)
                for k in range(2):
                    ins = nc.tensor.matmul(bank[k][:, 0:P], ones[:, :], diag[:, k, :], start=True, stop=True)
                ins.then_inc(max_rows, 1)
                pe.wait_ge(sum_edges, 1)
                nc.tensor.matmul(bank[2][:, 0:1], from_before[:, :], edge_val[:, 2:3], start=True, stop=True)
                nc.tensor.matmul(bank[2][:, 1:2], from_after[:, :], edge_val[:, 3:4], start=True,
                                 stop=True).then_inc(sum_carry, 1)

        with ExitStack() as ph:
            attrs = sb("attrs", [P, 2, G, DE], f32, ph)
            rows = sb("rows", [2, 2, G * P], bf16, ph)
            halves = sb("halves", [2, P], bf16, ph)
            cols = sb("cols", [P, NT], f32, ph)
            away = sb("away", [P, NT], f32, ph)
            high = sb("high", [P, NT], bf16, ph)
            low = sb("low", [P, NT], bf16, ph)
            iota_bf = sb("iota_bf", [P, P], bf16, ph)
            equal = sb("equal", [P, 2, G, P], f32, ph)
            earlier = sb("earlier", [P, G, P], f32, ph)
            n_earlier = sb("n_earlier", [P, G], f32, ph)
            move = sb("move", [P, G], f32, ph)
            add_idx = sb("add_idx", [P, 2, G], i32, ph)
            hot_high = sb("hot_high", [P, 2, G, J], bf16, ph)
            hot_low = sb("hot_low", [P, 2, G, P], bf16, ph)
            pair_sum = sb("pair_sum", [P, 2, 4 * P], f32, ph)
            project = sb("project", [P, 2, G, D], f32, ph)
            own_row = sb("own_row", [P, 1], f32, ph)
            cols_i = project[:, :, :, :].rearrange("p a b d -> p (a b d)")[:, 0:NT].bitcast(i32)
            dst_half = project[:, :, :, :].rearrange("p a b d -> p (a b d)")[:, 0:T].bitcast(i32)
            dst_i2 = equal[:, :, :, :].rearrange("p a b d -> p (a b d)")[:, 0:T].bitcast(i32)

            cols_in = sem("cols_in")
            consts = sem("consts")
            attrs_in = [sem(f"attrs_in{h}") for h in range(2)]
            rows_in = [sem(f"rows_in{h}") for h in range(2)]
            tail_clear = sem("tail_clear")
            rows_spread = sem("rows_spread")
            equal_ready = sem("equal_ready")
            idx_ready = sem("idx_ready")
            hots_ready = sem("hots_ready")
            group_done = sem("group_done")
            hist_taken = sem("hist_taken")
            pair_made = sem("pair_made")
            pair_copied = sem("pair_copied")
            pair_projected = sem("pair_projected")
            project_copied = sem("project_copied")
            adds_landed = sem("adds_landed")
            spare_rows_hit = G // K
            NPAIR = G // 2

            block = ph.enter_context(nc.Block("layer0"))

            def wait_added(engine, u):
                engine.wait_ge(adds_landed, after(u - 2))

            @block.sync
            def _(sp):
                sp.dma_start(cols_i, tile_src_cols).then_inc(cols_in, 16)
                sp.dma_start(dst_i2, dst_in).then_inc(cols_in, 16)

                def load(u, h):
                    sp.wait_ge(rows_spread, after(u - 2))
                    for part, of in enumerate((hi_line, lo_line)):
                        sp.dma_start(rows[part:part + 1, h, :],
                                     of[line(u * G * P, G * P)].rearrange("(a n) -> a n", a=1)
                                     ).then_inc(rows_in[h], 16)

                groups = edge_attr[0:U * G * P, :].rearrange("(u p b) f -> u p (b f)", p=P, b=G)
                with sp.Fori(0, PAIRS) as i:
                    for h in range(2):
                        u = 2 * i + h
                        load(u, h)
                        sp.wait_ge(group_done, after(u - 2))
                        sp.dma_start(attrs[:, h, :, :].rearrange("p b f -> p (b f)"),
                                     groups[line(u, 1), :, :].rearrange("u p f -> (u p) f")
                                     ).then_inc(attrs_in[h], 16)
                load(U, 0)
                sp.wait_ge(tail_clear, 1)
                sp.dma_start(attrs[0:LEFT, 0, 0, :], edge_attr[U * G * P:E, :]).then_inc(attrs_in[0], 16)

            @block.gpsimd
            def _(pool):
                pool.sem_inc(adds_landed, 1)

                def add_group(u, h, tiles):
                    pool.wait_ge(idx_ready, after(u))
                    for b in range(tiles):
                        k = b % K
                        if b % 2 == 0:
                            pool.wait_ge(project_copied, after(u * NPAIR + b // 2))
                        pool.wait_ge(added[k], 16 * (spare_rows_hit * u + b // K + 1))
                        pool.sem_inc(adds_landed if b == K else passed, 1)
                        nc.gpsimd.indirect_dma_start(
                            tables[k], bass.IndirectOffsetOnAxis(ap=add_idx[:, h, b:b + 1], axis=0),
                            project[:, h, b, :], None, compute_op=ALU.add).then_inc(added[k], 16)

                with pool.Fori(0, PAIRS) as i:
                    for h in range(2):
                        add_group(2 * i + h, h, G)
                add_group(U, 0, 1)
                for k in range(K):
                    pool.wait_ge(added[k], 16 * (spare_rows_hit * U + 1 + (k == 0)))

            @block.vector
            def _(dve):
                own = Vector(dve)
                for s in (equal_ready, idx_ready, hots_ready, hist_taken):
                    dve.sem_inc(s, 2)
                nc.vector.memset(halves[0:2, :], 1.0)
                nc.vector.memset(bank[4][:, 0:P], 0.0)
                own(nc.vector.tensor_copy(iota_bf[:, :], row_iota[:, :]))
                nc.vector.memset(halves[0:1, :], 128.0).then_inc(consts, 1)
                nc.vector.tensor_scalar(own_row[:, :], col_iota[:, :], float(NP), None, ALU.add)
                nc.vector.memset(high[:, :], 255.0)
                own(nc.vector.memset(low[:, :], 255.0))
                dve.wait_ge(cols_in, 32)
                own(nc.vector.tensor_copy(cols[:, :], cols_i))
                nc.vector.tensor_scalar(away[:, :], cols[:, :], -1.0, own_row[:, :], ALU.mult, ALU.add)
                own(nc.vector.tensor_scalar(dst_half, dst_i2, 7, None, ALU.logical_shift_right))
                own(nc.vector.tensor_copy(high[:, 0:T], dst_half))
                own(nc.vector.tensor_scalar(dst_half, dst_i2, 127, None, ALU.bitwise_and))
                own(nc.vector.tensor_copy(low[:, 0:T], dst_half))

                def take_hist(u):
                    dve.wait_ge(group_done, after(u))
                    nc.vector.tensor_tensor(hist[0:J, :], hist[0:J, :], bank[4][0:J, 0:P],
                                            ALU.add).then_inc(hist_taken, 1)

                def group(u, h):
                    here = line(u * G, G)
                    dve.wait_ge(rows_spread, after(u))
                    dve.wait_ge(group_done, after(u - 2))
                    nc.vector.tensor_tensor(
                        equal[:, h, :, :], row_bank[:, 0:G * P].rearrange("p (b q) -> p b q", q=P),
                        cols[:, here].unsqueeze(2).broadcast_to([P, G, P]), ALU.is_equal).then_inc(equal_ready, 1)
                    dve.wait_ge(equal_ready, after(u))
                    own(nc.vector.tensor_tensor(earlier[:, :, :], equal[:, h, :, :],
                                                lower[:, :].unsqueeze(1).broadcast_to([P, G, P]), ALU.mult))
                    own(nc.vector.reduce_sum(n_earlier[:, :], earlier[:, :, :], X_AXIS))
                    own(nc.vector.scalar_tensor_tensor(out=move[:, :], in0=n_earlier[:, :], scalar=0.0,
                                                       in1=away[:, here], op0=ALU.is_gt, op1=ALU.mult))
                    wait_added(dve, u)
                    nc.vector.tensor_tensor(add_idx[:, h, :], move[:, :], cols[:, here],
                                            ALU.add).then_inc(idx_ready, 1)
                    dve.wait_ge(group_done, after(u - 2))
                    nc.vector.tensor_tensor(hot_high[:, h, :, :],
                                            iota_bf[:, 0:J].unsqueeze(1).broadcast_to([P, G, J]),
                                            high[:, here].unsqueeze(2).broadcast_to([P, G, J]), ALU.is_equal)
                    nc.vector.tensor_tensor(hot_low[:, h, :, :],
                                            iota_bf[:, :].unsqueeze(1).broadcast_to([P, G, P]),
                                            low[:, here].unsqueeze(2).broadcast_to([P, G, P]),
                                            ALU.is_equal).then_inc(hots_ready, 1)
                    take_hist(u - 1)

                with dve.Fori(0, PAIRS) as i:
                    own.enter(i, 6)
                    for h in range(2):
                        group(2 * i + h, h)
                own.leave(PAIRS)
                dve.wait_ge(group_done, after(U - 2))
                nc.vector.memset(attrs[:, 0, 0, :], 0.0).then_inc(tail_clear, 1)
                group(U, 0)
                take_hist(U)
                own.close()

            @block.scalar
            def _(act):
                act.sem_inc(pair_copied, 2)
                act.sem_inc(project_copied, 2)

                def copy_pair(q, par, n):
                    act.wait_ge(pair_made, after(q))
                    act.wait_ge(pair_projected, after(q - 2))
                    nc.scalar.copy(pair_sum[:, par, 0:n * 2 * P], bank[par][:, 0:n * 2 * P]).then_inc(pair_copied, 1)

                def copy_project(q, par, h, k, n):
                    act.wait_ge(pair_projected, after(q))
                    nc.scalar.copy(project[:, h, 2 * k:2 * k + n, :].rearrange("p b d -> p (b d)"),
                                   bank[2 + par][:, 0:n * D]).then_inc(project_copied, 1)

                with act.Fori(0, PAIRS) as i:
                    for h in range(2):
                        u = 2 * i + h
                        for k in range(NPAIR):
                            copy_pair(u * NPAIR + k, (h * NPAIR + k) % 2, 2)
                            if k == 1:
                                wait_added(act, u)
                            if k:
                                copy_project(u * NPAIR + k - 1, (h * NPAIR + k - 1) % 2, h, k - 1, 2)
                        copy_project(u * NPAIR + NPAIR - 1, (h * NPAIR + NPAIR - 1) % 2, h, NPAIR - 1, 2)
                copy_pair(U * NPAIR, 0, 1)
                wait_added(act, U)
                copy_project(U * NPAIR, 0, 0, 0, 1)

            @block.tensor
            def _(pe):
                for s in (rows_spread, group_done, pair_made, pair_projected):
                    pe.sem_inc(s, 2)
                pe.wait_ge(consts, 1)

                def spread_rows(u, h, turn):
                    pe.wait_ge(rows_in[h], 32 * (turn + 1))
                    pe.wait_ge(equal_ready, after(u - 1))
                    for at in range(0, G * P, 512):
                        n = min(512, G * P - at)
                        ins = nc.tensor.matmul(row_bank[:, at:at + n], halves[0:2, :], rows[0:2, h, at:at + n],
                                               start=True, stop=True)
                    ins.then_inc(rows_spread, 1)

                def sum_pair(q, par, h, k, n):
                    pe.wait_ge(pair_copied, after(q - 2))
                    for t in range(n):
                        for c in range(2):
                            at = (2 * t + c) * P
                            ins = nc.tensor.matmul(bank[par][:, at:at + P],
                                                   attrs[:, h, 2 * k + t, c * P:(c + 1) * P],
                                                   equal[:, h, 2 * k + t, :], start=True, stop=True)
                    ins.then_inc(pair_made, 1)

                def project_pair(q, par, n):
                    pe.wait_ge(pair_copied, after(q))
                    pe.wait_ge(project_copied, after(q - 2))
                    for t in range(n):
                        for c in range(2):
                            at = (2 * t + c) * P
                            ins = nc.tensor.matmul(bank[2 + par][:, t * D:(t + 1) * D],
                                                   pair_sum[:, par, at:at + P], w0t[:, c, :],
                                                   start=(c == 0), stop=(c == 1))
                    ins.then_inc(pair_projected, 1)

                def add_hist(u, h):
                    pe.wait_ge(hots_ready, after(u))
                    pe.wait_ge(hist_taken, after(u))
                    for b in range(G):
                        ins = nc.tensor.matmul(bank[4][0:J, 0:P], hot_high[:, h, b, :], hot_low[:, h, b, :],
                                               start=(b == 0), stop=(b == G - 1))
                    ins.then_inc(group_done, 1)

                spread_rows(0, 0, 0)
                with pe.Fori(0, PAIRS) as i:
                    for h in range(2):
                        u = 2 * i + h
                        pe.wait_ge(attrs_in[h], 16 * (i + 1))
                        pe.wait_ge(equal_ready, after(u))
                        for k in range(NPAIR):
                            sum_pair(u * NPAIR + k, (h * NPAIR + k) % 2, h, k, 2)
                            if k == 0:
                                spread_rows(u + 1, 1 - h, i + h)
                            if k:
                                project_pair(u * NPAIR + k - 1, (h * NPAIR + k - 1) % 2, 2)
                        add_hist(u, h)
                        project_pair(u * NPAIR + NPAIR - 1, (h * NPAIR + NPAIR - 1) % 2, 2)
                pe.wait_ge(attrs_in[0], 16 * (PAIRS + 1))
                pe.wait_ge(equal_ready, after(U))
                sum_pair(U * NPAIR, 0, 0, 0, 1)
                add_hist(U, 0)
                project_pair(U * NPAIR, 0, 1)

        class Gather:

            def __init__(self, name, scope, width, used):
                self.rows = sb(f"{name}_rows", [P, 2, B, width], f32, scope)
                self.stage = sb(f"{name}_stage", [P, 2, B], i32, scope)
                self.staged = sem(f"{name}_staged")
                self.got = [sem(f"{name}_got{h}") for h in range(2)]
                self.used = used

            def pool(self, pool, table):
                with pool.Fori(0, TURNS) as i:
                    for h in range(2):
                        u = 2 * i + h
                        pool.wait_ge(self.staged, after(u))
                        pool.wait_ge(self.used, after(u - 2))
                        pool.sem_inc(passed, 1)
                        for b in range(B):
                            nc.gpsimd.indirect_dma_start(
                                self.rows[:, h, b, :], None, table,
                                bass.IndirectOffsetOnAxis(ap=self.stage[:, h, b:b + 1], axis=0)
                                ).then_inc(self.got[h], 16)

            def scalar_stage(self, act, idx, u, h):
                act.wait_ge(self.used, after(u - 2))
                nc.scalar.copy(self.stage[:, h, :], idx[:, line(u * B, B)]).then_inc(self.staged, 1)

            def wait_rows(self, engine, i, h):
                engine.wait_ge(self.got[h], 16 * B * (i + 1))

        class RunningSums:

            def __init__(self, name, scope):
                self.sums = sb(f"{name}_sums", [P, 2, B, D], f32, scope)
                self.carry = sb(f"{name}_carry", [P, D], f32, scope)
                self.summed = sem(f"{name}_summed")
                self.stored = [sem(f"{name}_stored{h}") for h in range(2)]
                self.carried = sem(f"{name}_carried")
                self.carry_copied = sem(f"{name}_carry_copied")
                self.whole = sem(f"{name}_whole")

            OWN = B - 1

            def vector_start(self, dve, own):
                dve.sem_inc(self.summed, 2)
                own(nc.vector.memset(self.sums[:, 1, B - 1, :], 0.0))

            def vector(self, dve, own, i, h, rows):
                u = 2 * i + h
                dve.wait_ge(self.stored[h], 16 * (i + 1))
                dve.wait_ge(self.summed, after(u - 1))
                for b in range(B):
                    before = self.sums[:, h, b - 1, :] if b else self.sums[:, 1 - h, B - 1, :]
                    ins = nc.vector.scalar_tensor_tensor(
                        out=self.sums[:, h, b, :], in0=before, scalar=same[:, line(u * B + b, 1)],
                        in1=rows(b), op0=ALU.mult, op1=ALU.add)
                    if b < B - 1:
                        own(ins)
                ins.then_inc(self.summed, 1)

            def sync_start(self, sp):
                for h in range(2):
                    sp.sem_inc(self.stored[h], 16)

            def sync(self, sp, i, h):
                u = 2 * i + h
                sp.wait_ge(self.summed, after(u))
                sp.dma_start(running_steps[:, line(u * B, B), :], self.sums[:, h, :, :]).then_inc(self.stored[h], 16)

            def tensor_carry(self, pe):
                pe.wait_ge(self.summed, after(2 * TURNS - 1))
                nc.tensor.matmul(bank[0][:, 0:D], from_before[:, :], self.sums[:, 1, B - 1, :],
                                 start=True, stop=True).then_inc(self.carried, 1)

            def vector_carry(self, dve):
                dve.wait_ge(self.carried, 1)
                nc.vector.tensor_copy(self.carry[:, :], bank[0][:, 0:D]).then_inc(self.carry_copied, 1)

            def pool_carry(self, pool):
                for h in range(2):
                    pool.wait_ge(self.stored[h], 16 * (TURNS + 1))
                pool.wait_ge(self.carry_copied, 1)
                nc.gpsimd.indirect_dma_start(
                    running, bass.IndirectOffsetOnAxis(ap=first_end[:, :], axis=0),
                    self.carry[:, :], None, compute_op=ALU.add).then_inc(self.whole, 16)

        class NodeSums:

            def __init__(self, name, scope):
                self.rows = sb(f"{name}_rows", [P, 2, JC, D], f32, scope)
                self.stage = sb(f"{name}_stage", [P, 2, JC], i32, scope)
                self.staged = sem(f"{name}_staged")
                self.got = [sem(f"{name}_got{h}") for h in range(2)]
                self.used = sem(f"{name}_used")

            def pool(self, pool, whole):
                with pool.Fori(0, NC // 2) as i:
                    for h in range(2):
                        c = 2 * i + h
                        pool.wait_ge(self.staged, after(c))
                        pool.wait_ge(self.used, after(c - 2))
                        pool.wait_ge(whole, 16)
                        pool.sem_inc(passed, 1)
                        for k in range(JC):
                            nc.gpsimd.indirect_dma_start(
                                self.rows[:, h, k, :], None, running,
                                bass.IndirectOffsetOnAxis(ap=self.stage[:, h, k:k + 1], axis=0)
                                ).then_inc(self.got[h], 16)

            def scalar_stage(self, act, c, h):
                act.wait_ge(self.used, after(c - 2))
                nc.scalar.copy(self.stage[:, h, :], node_row[:, line(c * JC, JC)]).then_inc(self.staged, 1)

            def wait_rows(self, engine, i, h):
                engine.wait_ge(self.got[h], 16 * JC * (i + 1))

        with ExitStack() as ph:
            part = sb("part", [P, 2, K, JC * D], f32, ph)
            hout = sb("hout", [P, 2, JC, D], f32, ph)
            line_cum = sb("line_cum", [P, P], f32, ph)
            hist_sum = sb("hist_sum", [P, 1], f32, ph)
            hist_off = sb("hist_off", [P, 1], f32, ph)
            cum = sb("cum", [P, J], f32, ph)
            has = sb("has", [P, J], f32, ph)
            has_row = sb("has_row", [P, 1], f32, ph)
            tmp = sb("tmp", [P, J], f32, ph)
            tmp2 = sb("tmp2", [P, J], f32, ph)
            dump = sb("dump", [P, J], f32, ph)
            hist_summed = sem("hist_summed")
            hist_offset = sem("hist_offset")
            cum_ready = sem("cum_ready")
            lines_stored = sem("lines_stored")
            lines_loaded = sem("lines_loaded")
            deg_floor = sem("deg_floor")
            deg_root = sem("deg_root")
            parts_in = [sem(f"parts_in{h}") for h in range(2)]
            parts_used = sem("parts_used")
            h_stored = [sem(f"h1_stored{h}") for h in range(2)]
            norm = Norm("norm1", ph)
            block = ph.enter_context(nc.Block("nodes1"))

            @block.sync
            def _(sp):
                for h in range(2):
                    sp.sem_inc(h_stored[h], 16)
                sp.wait_ge(cum_ready, 1)
                sp.dma_start(deg_line.rearrange("(a b) -> a b", b=P), hist[0:J, :]).then_inc(lines_stored, 16)
                sp.dma_start(cum_line.rearrange("(a b) -> a b", b=P), line_cum[0:J, :]).then_inc(lines_stored, 16)
                sp.wait_ge(lines_stored, 32)
                sp.dma_start(deg[:, :], deg_line.rearrange("(p j) -> p j", p=P)).then_inc(lines_loaded, 16)
                sp.dma_start(cum[:, :], cum_line.rearrange("(p j) -> p j", p=P)).then_inc(lines_loaded, 16)

                def load(c, h):
                    sp.wait_ge(parts_used, after(c - 2))
                    for k in range(K):
                        view = tables[k][0:NP, :].rearrange("(p j) d -> p (j d)", p=P)
                        sp.dma_start(part[:, h, k, :], view[:, line(c * JC * D, JC * D)]).then_inc(parts_in[h], 16)

                def store(i, h):
                    sp.wait_ge(norm.out_ready, 2 * i + h + 1)
                    sp.dma_start(h_columns[:, line((2 * i + h) * JC, JC), :], hout[:, h, :, :]
                                 ).then_inc(h_stored[h], 16)

                with sp.Fori(0, NC // 2) as i:
                    for h in range(2):
                        load(2 * i + h, h)
                    for h in range(2):
                        store(i, h)
                for h in range(2):
                    sp.wait_ge(h_stored[h], 16 * (NC // 2 + 1))

            @block.vector
            def _(dve):
                own = Vector(dve)
                dve.sem_inc(parts_used, 2)
                own(nc.vector.reduce_sum(hist_sum[:, :], hist[:, :], X_AXIS))
                nc.vector.tensor_tensor_scan(line_cum[:, :], ones[:, :], hist[:, :], 0.0, ALU.mult,
                                             ALU.add).then_inc(hist_summed, 1)
                dve.wait_ge(hist_summed, 1)
                dve.wait_ge(hist_offset, 1)
                own(nc.vector.tensor_copy(hist_off[:, :], bank[0][:, 0:1]))
                nc.vector.tensor_scalar(line_cum[:, :], line_cum[:, :], hist_off[:, :], None,
                                        ALU.add).then_inc(cum_ready, 1)
                dve.wait_ge(lines_loaded, 32)
                own(nc.vector.tensor_scalar(has[:, :], deg[:, :], 0.0, None, ALU.is_gt))
                nc.vector.tensor_scalar(tmp[:, :], deg[:, :], 1.0, None, ALU.max).then_inc(deg_floor, 1)
                dve.wait_ge(deg_root, 1)
                own(nc.vector.reciprocal(tmp[:, :], tmp2[:, :]))
                own(nc.vector.tensor_tensor(dinv[:, :], tmp[:, :], has[:, :], ALU.mult))
                own(nc.vector.tensor_scalar(tmp[:, :], cum[:, :], -1.0 - EP, None, ALU.add))
                own(nc.vector.tensor_tensor(tmp[:, :], tmp[:, :], has[:, :], ALU.mult))
                own(nc.vector.tensor_scalar(node_row[:, :], tmp[:, :], float(EP), None, ALU.add))
                own(nc.vector.tensor_scalar(has_row[:, :], col_iota[:, :], float(J), float(EP), ALU.mult, ALU.add))
                own(nc.vector.tensor_scalar(dump[:, :], row_iota[:, 0:J], has_row[:, :], None, ALU.add))
                own(nc.vector.tensor_tensor(tmp[:, :], cum[:, :], deg[:, :], ALU.subtract))
                own(nc.vector.tensor_tensor(tmp[:, :], tmp[:, :], dump[:, :], ALU.subtract))
                own(nc.vector.tensor_tensor(tmp[:, :], tmp[:, :], has[:, :], ALU.mult))
                own(nc.vector.tensor_tensor(node_start[:, :], tmp[:, :], dump[:, :], ALU.add))
                with dve.Fori(0, NC // 2) as i:
                    own.enter(i, 2 * (Norm.OWN + 1 + K - 1))
                    for h in range(2):
                        c = 2 * i + h
                        dve.wait_ge(parts_in[h], 16 * K * (i + 1))
                        flat = x[:, bass.ds(c * JC * D, JC * D)]
                        for k in range(K - 1):
                            own(nc.vector.tensor_tensor(flat, flat, part[:, h, k, :], ALU.add))
                        nc.vector.tensor_tensor(flat, flat, part[:, h, K - 1, :], ALU.add).then_inc(parts_used, 1)
                        dve.wait_ge(parts_used, after(c))
                        norm.vector(dve, own, c, lambda k: columns(c, k), dinv[:, line(c * JC, JC)])
                own.leave(NC // 2)
                own.close()

            @block.scalar
            def _(act):
                act.wait_ge(deg_floor, 1)
                nc.scalar.activation(tmp2[:, :], tmp[:, :], ACT.Sqrt).then_inc(deg_root, 1)
                with act.Fori(0, NC // 2) as i:
                    for h in range(2):
                        c = 2 * i + h
                        norm.scalar_std(act, c)
                        act.wait_ge(h_stored[h], 16 * (i + 1))
                        norm.scalar_apply(act, c, lambda k: columns(c, k), lambda k: hout[:, h, k, :], ACT.Relu)

            @block.tensor
            def _(pe):
                pe.wait_ge(hist_summed, 1)
                nc.tensor.matmul(bank[0][:, 0:1], upper[:, :], hist_sum[:, :], start=True,
                                 stop=True).then_inc(hist_offset, 1)

        def edge_layer(name, weights):
            with ExitStack() as ph:
                sums = RunningSums(f"{name}_run", ph)
                ring = Gather(f"{name}_ring", ph, D, sums.summed)
                block = ph.enter_context(nc.Block(name))

                @block.sync
                def _(sp):
                    sums.sync_start(sp)
                    with sp.Fori(0, TURNS) as i:
                        for h in range(2):
                            sums.sync(sp, i, h)

                @block.gpsimd
                def _(pool):
                    ring.pool(pool, h_table)
                    sums.pool_carry(pool)
                    pool.wait_ge(sums.whole, 16)

                @block.vector
                def _(dve):
                    own = Vector(dve)
                    sums.vector_start(dve, own)
                    with dve.Fori(0, TURNS) as i:
                        own.enter(i, 2 * (RunningSums.OWN + (weights is not None)))
                        for h in range(2):
                            ring.wait_rows(dve, i, h)
                            if weights is not None:
                                here = weights[:, line((2 * i + h) * B, B)]
                                own(nc.vector.tensor_tensor(
                                    ring.rows[:, h, :, :], ring.rows[:, h, :, :],
                                    here.unsqueeze(2).broadcast_to([P, B, D]), ALU.mult))
                            sums.vector(dve, own, i, h, lambda b: ring.rows[:, h, b, :])
                    own.leave(TURNS)
                    sums.vector_carry(dve)
                    own.close()

                @block.scalar
                def _(act):
                    act.sem_inc(ring.staged, 2)
                    with act.Fori(0, TURNS) as i:
                        for h in range(2):
                            ring.scalar_stage(act, src_idx, 2 * i + h, h)

                @block.tensor
                def _(pe):
                    sums.tensor_carry(pe)
                return sums

        layer1 = edge_layer("layer1", None)

        hn_scope = ExitStack()
        hn = sb("hn", [P, J, D], f32, hn_scope)

        def normed(c, k):
            return hn[:, line(c * JC + k, 1), :].rearrange("p a d -> p (a d)")

        with ExitStack() as ph:
            nodes = NodeSums("layer1_nodes", ph)
            h_stored = [sem(f"h2_stored{h}") for h in range(2)]
            norm = Norm("norm2", ph)
            block = ph.enter_context(nc.Block("nodes2"))

            @block.sync
            def _(sp):
                with sp.Fori(0, NC // 2) as i:
                    for h in range(2):
                        c = 2 * i + h
                        sp.wait_ge(norm.out_ready, c + 1)
                        sp.dma_start(h_columns[:, line(c * JC, JC), :], hn[:, line(c * JC, JC), :]
                                     ).then_inc(h_stored[h], 16)
                for h in range(2):
                    sp.wait_ge(h_stored[h], 16 * (NC // 2))

            @block.gpsimd
            def _(pool):
                nodes.pool(pool, layer1.whole)

            @block.vector
            def _(dve):
                own = Vector(dve)
                dve.sem_inc(nodes.used, 2)
                with dve.Fori(0, NC // 2) as i:
                    own.enter(i, 2 * (1 + Norm.OWN))
                    for h in range(2):
                        c = 2 * i + h
                        nodes.wait_rows(dve, i, h)
                        own(nc.vector.tensor_tensor(
                            nodes.rows[:, h, :, :], nodes.rows[:, h, :, :],
                            dinv[:, line(c * JC, JC)].unsqueeze(2).broadcast_to([P, JC, D]), ALU.mult))
                        nc.vector.tensor_tensor(chunk(c), chunk(c), nodes.rows[:, h, :, :],
                                                ALU.add).then_inc(nodes.used, 1)
                        dve.wait_ge(nodes.used, after(c))
                        norm.vector(dve, own, c, lambda k: columns(c, k))
                own.leave(NC // 2)
                own.close()

            @block.scalar
            def _(act):
                act.sem_inc(nodes.staged, 2)
                with act.Fori(0, NC // 2) as i:
                    for h in range(2):
                        c = 2 * i + h
                        nodes.scalar_stage(act, c, h)
                        norm.scalar_std(act, c)
                        norm.scalar_apply(act, c, lambda k: columns(c, k), lambda k: normed(c, k), ACT.Relu)

        layer2 = edge_layer("layer2", ew_prob)

        with ExitStack() as ph:
            nodes = NodeSums("layer2_nodes", ph)
            square = sb("square", [P, JC, D], f32, ph)
            sumsq = sb("sumsq", [P, JC], f32, ph)
            length = sb("length", [P, JC], f32, ph)
            inverse = sb("inverse", [P, JC], f32, ph)
            turned = sb("turned", [P, 2, 2 * P], f32, ph)
            hn_here = sb("hn_here", [P, JC, D], f32, ph)
            comb = sb("comb", [P, JC, D], f32, ph)
            hrel = square
            hrel_turned = sb("hrel_turned", [P, 2, P], f32, ph)
            rel_rows = sb("rel_rows", [P, 2, JC, R, XW], f32, ph)
            adst_rows = sb("adst_rows", [P, 2, JC, RH], f32, ph)
            start_stage = sb("start_stage", [P, 2, JC], i32, ph)
            adst_first = sb("adst_first", [P, RH], f32, ph)
            agg_scaled = sem("agg_scaled")
            hn_placed = sem("hn_placed")
            sumsq_ready = sem("sumsq_ready")
            length_ready = sem("length_ready")
            nodes_turned = sem("nodes_turned")
            turned_copied = sem("turned_copied")
            combined = sem("combined")
            comb_copied = sem("comb_copied")
            h_turned = sem("h_turned")
            h_turned_copied = sem("h_turned_copied")
            projected = sem("projected")
            rel_copied = sem("rel_copied")
            scores_copied = sem("scores_copied")
            start_staged = sem("start_staged")
            rel_stored = [sem(f"rel_stored{h}") for h in range(2)]
            adst_stored = [sem(f"adst_stored{h}") for h in range(2)]
            spread = [sem(f"spread{h}") for h in range(2)]
            spread_landed = sem("spread_landed")
            first_got = sem("first_got")
            first_put = sem("first_put")
            comb_norm = Norm("norm_comb", ph)
            norm = Norm("norm3", ph)
            block = ph.enter_context(nc.Block("nodes3"))

            @block.sync
            def _(sp):
                for h in range(2):
                    sp.sem_inc(rel_stored[h], 16)
                    sp.sem_inc(adst_stored[h], 16)
                with sp.Fori(0, NC // 2) as i:
                    for h in range(2):
                        c = 2 * i + h
                        sp.wait_ge(rel_copied, after((c + 1) * JC - 1))
                        sp.wait_ge(scores_copied, after((c + 1) * JC - 1))
                        sp.dma_start(rel_columns[:, line(c * JC, JC), :, :].rearrange("p j r d -> p (j r d)"),
                                     rel_rows[:, h, :, :, :].rearrange("p j r d -> p (j r d)")
                                     ).then_inc(rel_stored[h], 16)
                        sp.dma_start(adst_columns[:, line(c * JC, JC), :], adst_rows[:, h, :, :]
                                     ).then_inc(adst_stored[h], 16)
                for h in range(2):
                    sp.wait_ge(rel_stored[h], 16 * (NC // 2 + 1))
                sp.wait_ge(first_got, 16)
                for h in range(2):
                    sp.wait_ge(spread[h], 16 * JC * (NC // 2))
                sp.dma_start(adst_steps[:, 0, :], adst_first[:, :]).then_inc(first_put, 16)
                sp.wait_ge(first_put, 16)

            @block.gpsimd
            def _(pool):
                pool.sem_inc(spread_landed, 1)
                with pool.Fori(0, NC // 2) as i:
                    for h in range(2):
                        c = 2 * i + h
                        pool.wait_ge(nodes.staged, after(c))
                        pool.wait_ge(nodes.used, after(c - 2))
                        pool.wait_ge(layer2.whole, 16)
                        pool.sem_inc(passed, 1)
                        for k in range(JC):
                            nc.gpsimd.indirect_dma_start(
                                nodes.rows[:, h, k, :], None, running,
                                bass.IndirectOffsetOnAxis(ap=nodes.stage[:, h, k:k + 1], axis=0)
                                ).then_inc(nodes.got[h], 16)
                    for h in range(2):
                        c = 2 * i + h
                        pool.wait_ge(start_staged, after(c))
                        pool.wait_ge(scores_copied, after((c + 1) * JC - 1))
                        pool.sem_inc(passed, 1)
                        for k in range(JC):
                            nc.gpsimd.indirect_dma_start(
                                adst_edges, bass.IndirectOffsetOnAxis(ap=start_stage[:, h, k:k + 1], axis=0),
                                adst_rows[:, h, k, :], None).then_inc(spread[h], 16)
                    for h in range(2):
                        pool.wait_ge(spread[h], 16 * JC * (i + 1))
                    pool.sem_inc(spread_landed, 1)
                for h in range(2):
                    pool.wait_ge(adst_stored[h], 16 * (NC // 2 + 1))
                nc.gpsimd.indirect_dma_start(
                    adst_first[:, :], None, adst_nodes,
                    bass.IndirectOffsetOnAxis(ap=first_node[:, :], axis=0)).then_inc(first_got, 16)

            @block.vector
            def _(dve):
                own = Vector(dve)
                for s in (nodes.used, comb_copied, scores_copied):
                    dve.sem_inc(s, 2)
                with dve.Fori(0, NC // 2) as i:
                    own.enter(i, 2 * (2 * 3 + 1 + Norm.OWN + 2 + Norm.OWN))
                    for h in range(2):
                        c = 2 * i + h

                        def reciprocal_length(n, of):
                            own(nc.vector.tensor_tensor(square[:, :, :], of, of, ALU.mult))
                            nc.vector.reduce_sum(sumsq[:, :], square[:, :, :], X_AXIS).then_inc(sumsq_ready, 1)
                            dve.wait_ge(length_ready, 2 * c + n + 1)
                            own(nc.vector.tensor_scalar(inverse[:, :], length[:, :], NORM_EPS, None, ALU.add))
                            own(nc.vector.reciprocal(inverse[:, :], inverse[:, :]))
                            return inverse[:, :].unsqueeze(2).broadcast_to([P, JC, D])

                        nodes.wait_rows(dve, i, h)
                        agg = nodes.rows[:, h, :, :]
                        nc.vector.tensor_tensor(agg, agg, reciprocal_length(0, agg),
                                                ALU.mult).then_inc(agg_scaled, 1)
                        for k in range(JC):
                            q = c * JC + k
                            dve.wait_ge(combined, after(q))
                            ins = nc.vector.scalar_tensor_tensor(
                                out=comb[:, k, :], in0=bank[2][:, 0:D], scalar=0.5, in1=half_bias[:, :],
                                op0=ALU.mult, op1=ALU.add)
                            ins.then_inc(comb_copied, 1)
                        dve.wait_ge(comb_copied, after((c + 1) * JC - 1))
                        by = reciprocal_length(1, comb[:, :, :])
                        own(nc.vector.tensor_tensor(comb[:, :, :], comb[:, :, :], by, ALU.mult))
                        comb_norm.vector(dve, own, c, lambda k: comb[:, k, :])
                        dve.wait_ge(comb_norm.out_ready, c + 1)
                        own(nc.vector.tensor_tensor(comb[:, :, :], comb[:, :, :],
                                                    gamma[:, :].unsqueeze(1).broadcast_to([P, JC, D]), ALU.mult))
                        own(nc.vector.tensor_tensor(comb[:, :, :], comb[:, :, :],
                                                    beta[:, :].unsqueeze(1).broadcast_to([P, JC, D]), ALU.add))
                        nc.vector.tensor_tensor(chunk(c), chunk(c), comb[:, :, :], ALU.add).then_inc(nodes.used, 1)
                        dve.wait_ge(nodes.used, after(c))
                        norm.vector(dve, own, c, lambda k: columns(c, k))
                        dve.wait_ge(rel_stored[h], 16 * (i + 1))
                        dve.wait_ge(adst_stored[h], 16 * (i + 1))
                        dve.wait_ge(spread_landed, i + 1)
                        for k in range(JC):
                            q = c * JC + k
                            dve.wait_ge(projected, after(q))
                            nc.vector.tensor_copy(rel_rows[:, h, k, :, D:XW],
                                                  bank[4][:, 0:RH].rearrange("p (r h) -> p r h", r=R))
                            nc.vector.tensor_copy(adst_rows[:, h, k, :],
                                                  bank[4][:, RH:2 * RH]).then_inc(scores_copied, 1)
                own.leave(NC // 2)
                own.close()

            @block.scalar
            def _(act):
                for s in (nodes.staged, start_staged, turned_copied, h_turned_copied, rel_copied):
                    act.sem_inc(s, 2)

                def root_of_sumsq(n):
                    act.wait_ge(sumsq_ready, n + 1)
                    nc.scalar.activation(length[:, :], sumsq[:, :], ACT.Sqrt).then_inc(length_ready, 1)

                with act.Fori(0, NC // 2) as i:
                    for h in range(2):
                        nodes.scalar_stage(act, 2 * i + h, h)
                    for h in range(2):
                        c = 2 * i + h
                        act.wait_ge(spread_landed, i + 1)
                        nc.scalar.copy(start_stage[:, h, :], node_start[:, line(c * JC, JC)]
                                       ).then_inc(start_staged, 1)
                        nc.scalar.copy(hn_here[:, :, :], hn[:, line(c * JC, JC), :]).then_inc(hn_placed, 1)
                        root_of_sumsq(2 * c)
                        for k in range(JC):
                            q = c * JC + k
                            act.wait_ge(nodes_turned, after(q))
                            act.wait_ge(combined, after(q - 2))
                            nc.scalar.copy(turned[:, (h * JC + k) % 2, :], bank[(h * JC + k) % 2][:, 0:2 * P]).then_inc(turned_copied, 1)
                        root_of_sumsq(2 * c + 1)
                        comb_norm.scalar_std(act, c)
                        comb_norm.scalar_apply(act, c, lambda k: comb[:, k, :], lambda k: comb[:, k, :],
                                               ACT.Identity)
                        norm.scalar_std(act, c)
                        norm.scalar_apply(act, c, lambda k: columns(c, k), lambda k: hrel[:, k, :], ACT.Relu)
                        act.wait_ge(rel_stored[h], 16 * (i + 1))
                        for k in range(JC):
                            q = c * JC + k
                            act.wait_ge(h_turned, after(q))
                            act.wait_ge(projected, after(q - 1))
                            nc.scalar.copy(hrel_turned[:, (h * JC + k) % 2, :], bank[(h * JC + k) % 2][:, 256:256 + P]
                                           ).then_inc(h_turned_copied, 1)
                            act.wait_ge(projected, after(q))
                            nc.scalar.copy(rel_rows[:, h, k, :, 0:D],
                                           bank[3][:, :].rearrange("p (r d) -> p r d", r=R)
                                           ).then_inc(rel_copied, 1)

            @block.tensor
            def _(pe):
                for s in (nodes_turned, combined, h_turned, projected):
                    pe.sem_inc(s, 2)
                with pe.Fori(0, NC // 2) as i:
                    for h in range(2):
                        c = 2 * i + h
                        pe.wait_ge(agg_scaled, c + 1)
                        pe.wait_ge(hn_placed, c + 1)
                        for k in range(JC):
                            q = c * JC + k
                            pe.wait_ge(turned_copied, after(q - 2))
                            nc.tensor.transpose(bank[(h * JC + k) % 2][:, 0:P], nodes.rows[:, h, k, :], ident[:, :])
                            nc.tensor.transpose(bank[(h * JC + k) % 2][:, P:2 * P], hn_here[:, k, :],
                                                ident[:, :]).then_inc(nodes_turned, 1)
                            pe.wait_ge(turned_copied, after(q))
                            pe.wait_ge(comb_copied, after(q - 1))
                            nc.tensor.matmul(bank[2][:, 0:D], turned[:, (h * JC + k) % 2, 0:P], wnb[:, :],
                                             start=True, stop=False)
                            nc.tensor.matmul(bank[2][:, 0:D], turned[:, (h * JC + k) % 2, P:2 * P], wself[:, :],
                                             start=False, stop=True).then_inc(combined, 1)
                        pe.wait_ge(norm.out_ready, c + 1)
                        for k in range(JC):
                            q = c * JC + k
                            pe.wait_ge(h_turned_copied, after(q - 2))
                            nc.tensor.transpose(bank[(h * JC + k) % 2][:, 256:256 + P], hrel[:, k, :],
                                                ident[:, :]).then_inc(h_turned, 1)
                            pe.wait_ge(h_turned_copied, after(q))
                            pe.wait_ge(rel_copied, after(q - 1))
                            pe.wait_ge(scores_copied, after(q - 1))
                            nc.tensor.matmul(bank[3][:, :], hrel_turned[:, (h * JC + k) % 2, :], w3[:, :],
                                             start=True, stop=True)
                            nc.tensor.matmul(bank[4][:, 0:2 * RH], hrel_turned[:, (h * JC + k) % 2, :], w3_score[:, :],
                                             start=True, stop=True).then_inc(projected, 1)
        hn_scope.close()

        with ExitStack() as ph:
            score = sb("score", [P, H, T], f32, ph)

            with ExitStack() as sub:
                scores_taken = sem("scores_taken")
                kept = [sem(f"kept{h}") for h in range(2)]
                ring = Gather("layer3_ring", sub, XW, scores_taken)
                S = 2 * B
                adst_in = sb("adst_in", [P, 2, S, RH], f32, sub)
                fill = sb("fill", [P, RH, S], f32, sub)
                fill_last = sb("fill_last", [P, RH], f32, sub)
                fill_typed = sb("fill_typed", [P, R, H, S], f32, sub)
                adst_own = sb("adst_own", [P, H, S], f32, sub)
                adst_loaded = [sem(f"adst_loaded{h}") for h in range(2)]
                scores_moved = sem("scores_moved")
                scores_made = sem("scores_made")
                block = sub.enter_context(nc.Block("layer3_scores"))
                assert TURNS % 2 == 0

                @block.sync
                def _(sp):
                    for h in range(2):
                        sp.sem_inc(kept[h], 16)
                    with sp.Fori(0, TURNS // 2) as ii:
                        for g in range(2):
                            i = 2 * ii + g
                            sp.wait_ge(scores_made, after(i - 2))
                            sp.dma_start(adst_in[:, g, :, :], adst_steps[:, line(i * S, S), :]
                                         ).then_inc(adst_loaded[g], 16)
                            for h in range(2):
                                sp.wait_ge(ring.got[h], 16 * B * (i + 1))
                                sp.dma_start(rel_steps[:, line((2 * i + h) * B, B), :], ring.rows[:, h, :, :]
                                             ).then_inc(kept[h], 16)
                    for h in range(2):
                        sp.wait_ge(kept[h], 16 * (TURNS + 1))

                @block.gpsimd
                def _(pool):
                    with pool.Fori(0, TURNS) as i:
                        for h in range(2):
                            u = 2 * i + h
                            pool.wait_ge(ring.staged, after(u))
                            pool.wait_ge(scores_taken, after(u - 2))
                            pool.wait_ge(kept[h], 16 * (i + 1))
                            pool.sem_inc(passed, 1)
                            for b in range(B):
                                nc.gpsimd.indirect_dma_start(
                                    ring.rows[:, h, b, :], None, rel_table,
                                    bass.IndirectOffsetOnAxis(ap=ring.stage[:, h, b:b + 1], axis=0)
                                    ).then_inc(ring.got[h], 16)

                @block.scalar
                def _(act):
                    act.sem_inc(ring.staged, 2)
                    act.sem_inc(scores_taken, 2)

                    def stage(u, h):
                        act.wait_ge(scores_taken, after(u - 2))
                        nc.scalar.copy(ring.stage[:, h, :], rel_idx[:, line(u * B, B)]).then_inc(ring.staged, 1)

                    def take(i, h):
                        u = 2 * i + h
                        ring.wait_rows(act, i, h)
                        nc.scalar.copy(score[:, :, line(u * B, B)],
                                       ring.rows[:, h, :, D:XW].rearrange("p b h -> p h b")
                                       ).then_inc(scores_taken, 1)

                    stage(0, 0)
                    stage(1, 1)
                    with act.Fori(0, TURNS - 1) as i:
                        for h in range(2):
                            take(i, h)
                            act.wait_ge(scores_taken, after(2 * i + h))
                            act.wait_ge(kept[h], 16 * (i + 2))
                            nc.scalar.copy(ring.stage[:, h, :], rel_idx[:, line((2 * i + 2 + h) * B, B)]
                                           ).then_inc(ring.staged, 1)
                    for h in range(2):
                        take(TURNS - 1, h)

                @block.vector
                def _(dve):
                    own = Vector(dve)
                    dve.sem_inc(scores_made, 2)
                    own(nc.vector.memset(fill_last[:, :], 0.0))
                    with dve.Fori(0, TURNS // 2) as ii:
                        own.enter(ii, 2 * 5)
                        for g in range(2):
                            i = 2 * ii + g
                            steps = line(i * S, S)
                            dve.wait_ge(adst_loaded[g], 16 * (ii + 1))
                            for k in range(RH):
                                ins = nc.vector.tensor_tensor_scan(
                                    fill[:, k, :], same[:, steps], adst_in[:, g, :, k],
                                    fill_last[:, k:k + 1], ALU.mult, ALU.add)
                            own(ins)
                            own(nc.vector.tensor_copy(fill_last[:, :], fill[:, :, S - 1]))
                            for r in range(R):
                                ins = nc.vector.tensor_tensor(
                                    fill_typed[:, r, :, :], fill[:, r * H:(r + 1) * H, :],
                                    is_type[:, r, steps].unsqueeze(1).broadcast_to([P, H, S]), ALU.mult)
                            own(ins)
                            own(nc.vector.tensor_reduce(
                                adst_own[:, :, :], fill_typed[:, :, :, :].rearrange("p r h s -> p h s r"),
                                X_AXIS, ALU.add))
                            dve.wait_ge(scores_taken, after(2 * i + 1))
                            here = score[:, :, steps]
                            own(nc.vector.tensor_tensor(here, here, adst_own[:, :, :], ALU.add))
                            nc.vector.scalar_tensor_tensor(out=here, in0=here, scalar=SLOPE, in1=here,
                                                           op0=ALU.mult, op1=ALU.max).then_inc(scores_made, 1)
                            dve.wait_ge(scores_made, after(i))
                    own.leave(TURNS // 2)
                    own.close()

            with ExitStack() as sub:
                most = sb("most", [P, H, T], f32, sub)
                scan_a = sb("scan_a3", [P, T], f32, sub)
                scan_b = sb("scan_b3", [P, T], f32, sub)
                limit = sb("limit", [P, T], f32, sub)
                neg = sb("neg3", [P, T + 1], f32, sub)
                ends = sb("ends", [P, RH, 2], f32, sub)
                diag = sb("diag3", [P, 2, 4, P], f32, sub)
                masked = sb("masked3", [P, 4, P], f32, sub)
                other = sb("other", [P, RH, 2], f32, sub)
                diag_ready = sem("diag3_ready")
                rows_made = sem("rows3_made")
                shifted = sem("shifted")
                exp_made = sem("exp_made")
                ends_ready = sem("ends_ready")
                others_made = sem("others_made")
                block = sub.enter_context(nc.Block("layer3_softmax"))
                CG = RH // 4

                @block.vector
                def _(dve):
                    own = Vector(dve)
                    own(nc.vector.tensor_scalar(neg[:, :], same[:, :], -1.0, BIG, ALU.add, ALU.mult))
                    for r in range(R):
                        own(nc.vector.tensor_scalar(limit[:, :], is_type[:, r, :], -0.5, 2 * BIG, ALU.add, ALU.mult))
                        for h in range(H):
                            k = r * H + h
                            own(nc.vector.tensor_tensor(scan_a[:, :], score[:, h, :], limit[:, :], ALU.min))
                            own(nc.vector.tensor_tensor_scan(scan_b[:, :], neg[:, 0:T], scan_a[:, :], 0.0,
                                                             ALU.add, ALU.max))
                            own(nc.vector.tensor_copy(ends[:, k, 1:2], scan_b[:, T - 1:T]))
                            own(nc.vector.tensor_tensor_scan(scan_a[:, ::-1], neg[:, 1:T + 1][:, ::-1],
                                                             scan_b[:, ::-1], 0.0, ALU.add, ALU.max))
                            own(nc.vector.tensor_copy(ends[:, k, 0:1], scan_a[:, 0:1]))
                            if r == 0:
                                own(nc.vector.tensor_tensor(most[:, h, :], scan_a[:, :], is_type[:, r, :], ALU.mult))
                            else:
                                own(nc.vector.tensor_tensor(scan_b[:, :], scan_a[:, :], is_type[:, r, :], ALU.mult))
                                own(nc.vector.tensor_tensor(most[:, h, :], most[:, h, :], scan_b[:, :], ALU.add))
                    for g in range(CG):
                        for side in range(2):
                            for k in range(4):
                                ins = nc.vector.tensor_scalar(diag[:, side, k, :], ident[:, :],
                                                              ends[:, 4 * g + k, 1 - side:2 - side], None, ALU.mult)
                        ins.then_inc(diag_ready, 1)
                        dve.wait_ge(rows_made, g + 1)
                        for side, bias in enumerate((bias_before, bias_after)):
                            own(nc.vector.tensor_tensor(
                                masked[:, :, :], bank[side][:, :].rearrange("p (k q) -> p k q", q=P),
                                bias[:, :].unsqueeze(1).broadcast_to([P, 4, P]), ALU.add))
                            own(nc.vector.tensor_reduce(other[:, 4 * g:4 * g + 4, side], masked[:, :, :],
                                                        X_AXIS, ALU.max))
                    for side, mask in enumerate((first, last)):
                        for r in range(R):
                            own(nc.vector.tensor_tensor(scan_a[:, :], mask[:, :], is_type[:, r, :], ALU.mult))
                            own(nc.vector.tensor_scalar(scan_a[:, :], scan_a[:, :], -1.0, BIG, ALU.add, ALU.mult))
                            for h in range(H):
                                ins = nc.vector.scalar_tensor_tensor(
                                    out=most[:, h, :], in0=scan_a[:, :], scalar=other[:, r * H + h, side:side + 1],
                                    in1=most[:, h, :], op0=ALU.add, op1=ALU.max)
                            own(ins)
                    nc.vector.tensor_tensor(score[:, :, :], score[:, :, :], most[:, :, :],
                                            ALU.subtract).then_inc(shifted, 1)
                    dve.wait_ge(exp_made, 1)
                    for r in range(R):
                        for h in range(H):
                            k = r * H + h
                            own(nc.vector.tensor_tensor(scan_a[:, :], score[:, h, :], is_type[:, r, :], ALU.mult))
                            own(nc.vector.tensor_tensor_scan(scan_b[:, :], same[:, 0:T], scan_a[:, :], 0.0,
                                                             ALU.mult, ALU.add))
                            own(nc.vector.tensor_copy(ends[:, k, 1:2], scan_b[:, T - 1:T]))
                            own(nc.vector.scalar_tensor_tensor(out=scan_a[:, :], in0=same[:, 1:T + 1], scalar=1.0,
                                                               in1=scan_b[:, :], op0=ALU.is_lt, op1=ALU.mult))
                            own(nc.vector.tensor_tensor_scan(scan_b[:, ::-1], same[:, 1:T + 1][:, ::-1],
                                                             scan_a[:, ::-1], 0.0, ALU.mult, ALU.add))
                            own(nc.vector.tensor_copy(ends[:, k, 0:1], scan_b[:, 0:1]))
                            if r == 0:
                                own(nc.vector.tensor_tensor(most[:, h, :], scan_b[:, :], is_type[:, r, :], ALU.mult))
                            else:
                                own(nc.vector.tensor_tensor(scan_a[:, :], scan_b[:, :], is_type[:, r, :], ALU.mult))
                                own(nc.vector.tensor_tensor(most[:, h, :], most[:, h, :], scan_a[:, :], ALU.add))
                    nc.vector.tensor_copy(masked[:, 0, 0:2 * RH], ends[:, :, :].rearrange("p k s -> p (k s)")
                                          ).then_inc(ends_ready, 1)
                    dve.wait_ge(others_made, 1)
                    for side in range(2):
                        own(nc.vector.tensor_copy(other[:, :, side], bank[2 + side][:, 0:RH]))
                    for side, mask in enumerate((first, last)):
                        for r in range(R):
                            own(nc.vector.tensor_tensor(scan_a[:, :], mask[:, :], is_type[:, r, :], ALU.mult))
                            for h in range(H):
                                ins = nc.vector.scalar_tensor_tensor(
                                    out=most[:, h, :], in0=scan_a[:, :], scalar=other[:, r * H + h, side:side + 1],
                                    in1=most[:, h, :], op0=ALU.mult, op1=ALU.add)
                            own(ins)
                    own(nc.vector.reciprocal(most[:, :, :], most[:, :, :]))
                    own(nc.vector.tensor_tensor(score[:, :, :], score[:, :, :], most[:, :, :], ALU.mult))
                    own.close()

                @block.scalar
                def _(act):
                    act.wait_ge(shifted, 1)
                    nc.scalar.activation(score[:, :, :], score[:, :, :], ACT.Exp).then_inc(exp_made, 1)

                @block.tensor
                def _(pe):
                    for g in range(CG):
                        pe.wait_ge(diag_ready, g + 1)
                        for side in range(2):
                            ins = nc.tensor.matmul(bank[side][:, :], ones[:, :],
                                                   diag[:, side, :, :].rearrange("p k q -> p (k q)"),
                                                   start=True, stop=True)
                        ins.then_inc(rows_made, 1)
                    pe.wait_ge(ends_ready, 1)
                    for side, mask in enumerate((from_before, from_after)):
                        ins = nc.tensor.matmul(bank[2 + side][:, 0:RH], mask[:, :], ends[:, :, 1 - side],
                                               start=True, stop=True)
                    ins.then_inc(others_made, 1)

            with ExitStack() as sub:
                sums = RunningSums("layer3_run", sub)
                rel_rows = sb("rel_rows3", [P, 2, B, XW], f32, sub)
                message = sb("message", [P, B, D], f32, sub)
                rel_in = [sem(f"rel_in{h}") for h in range(2)]
                block = sub.enter_context(nc.Block("layer3_sums"))

                @block.sync
                def _(sp):
                    sums.sync_start(sp)

                    def load(i, h):
                        sp.wait_ge(sums.summed, after(2 * i + h - 2))
                        sp.dma_start(rel_rows[:, h, :, :], rel_steps[:, line((2 * i + h) * B, B), :]
                                     ).then_inc(rel_in[h], 16)

                    for h in range(2):
                        load(0, h)
                    with sp.Fori(0, TURNS - 1) as i:
                        for h in range(2):
                            sums.sync(sp, i, h)
                            load(i + 1, h)
                    for h in range(2):
                        sums.sync(sp, TURNS - 1, h)

                @block.gpsimd
                def _(pool):
                    sums.pool_carry(pool)
                    pool.wait_ge(sums.whole, 16)

                @block.vector
                def _(dve):
                    own = Vector(dve)
                    sums.vector_start(dve, own)
                    with dve.Fori(0, TURNS) as i:
                        own.enter(i, 2 * (RunningSums.OWN + 1))
                        for h in range(2):
                            dve.wait_ge(rel_in[h], 16 * (i + 1))
                            dve.wait_ge(sums.summed, after(2 * i + h - 1))
                            here = score[:, :, line((2 * i + h) * B, B)].rearrange("p h b -> p b h")
                            own(nc.vector.tensor_tensor(
                                message[:, :, :].rearrange("p b (h d) -> p b h d", d=HD),
                                rel_rows[:, h, :, 0:D].rearrange("p b (h d) -> p b h d", d=HD),
                                here.unsqueeze(3).broadcast_to([P, B, H, HD]), ALU.mult))
                            sums.vector(dve, own, i, h, lambda b: message[:, b, :])
                    own.leave(TURNS)
                    sums.vector_carry(dve)
                    own.close()

                @block.tensor
                def _(pe):
                    sums.tensor_carry(pe)
                layer3 = sums

        with ExitStack() as ph:
            nodes = NodeSums("layer3_nodes", ph)
            stored = sem("out_stored")
            block = ph.enter_context(nc.Block("nodes4"))

            @block.sync
            def _(sp):
                sp.wait_ge(nodes.used, after(NC - 1))
                whole = N // J
                stores = 0
                for a, b in ((0, whole // 16 * 16), (whole // 16 * 16, whole)):
                    if b > a:
                        sp.dma_start(out[a * J:b * J, :].rearrange("(p j) d -> p (j d)", j=J),
                                     x[a:b, :]).then_inc(stored, 16)
                        stores += 1
                rest = N - whole * J
                if rest:
                    sp.dma_start(out[whole * J:N, :].rearrange("(a j) d -> a (j d)", a=1),
                                 x[whole:whole + 1, 0:rest * D]).then_inc(stored, 16)
                    stores += 1
                sp.wait_ge(stored, 16 * stores)

            @block.gpsimd
            def _(pool):
                nodes.pool(pool, layer3.whole)

            @block.vector
            def _(dve):
                own = Vector(dve)
                dve.sem_inc(nodes.used, 2)
                with dve.Fori(0, NC // 2) as i:
                    own.enter(i, 0)
                    for h in range(2):
                        c = 2 * i + h
                        nodes.wait_rows(dve, i, h)
                        nc.vector.tensor_tensor(chunk(c), chunk(c), nodes.rows[:, h, :, :],
                                                ALU.add).then_inc(nodes.used, 1)
                own.leave(NC // 2)
                own.close()

            @block.scalar
            def _(act):
                act.sem_inc(nodes.staged, 2)
                with act.Fori(0, NC // 2) as i:
                    for h in range(2):
                        nodes.scalar_stage(act, 2 * i + h, h)


_INS = ["x", "src", "dst", "edge_type", "edge_weight", "tile_src", "tile_src_cols", "edge_attr", "w0", "b0",
        "w_self", "w_nb", "b_self", "b_nb", "gamma", "beta", "w3", "attn"]


def lay_out(x, src, dst, edge_attr_256, edge_type_4, edge_weight, L0_gnn_W, L0_gnn_b, L2_gnn_W_self,
            L2_gnn_b_self, L2_gnn_W_nb, L2_gnn_b_nb, L2_gnn_gamma, L2_gnn_beta, L3_gnn_W, L3_gnn_attn):
    import numpy as np

    x, src, dst = np.asarray(x), np.asarray(src), np.asarray(dst)
    n, e = x.shape[0], src.shape[0]
    j, t = node_columns(n), steps_per_partition(e)
    groups = 2 * (e // (2 * G * P))
    tiles = (groups + 1) * G

    def padded(a, size, value):
        return np.concatenate([a, np.full((size - a.shape[0],) + a.shape[1:], value, a.dtype)])

    def by_partition(a, value):
        return np.ascontiguousarray(padded(np.asarray(a), P * t, value).reshape(P, t))

    def on_all(a):
        return np.ascontiguousarray(np.broadcast_to(np.asarray(a).reshape(1, -1), (P, a.size)))

    pad_node = P * j - 1
    order = src[:groups * G * P].reshape(groups, P, G).transpose(0, 2, 1).reshape(-1)
    tile_src = padded(np.concatenate([order, src[groups * G * P:]]), tiles * P, pad_node)
    attn = np.asarray(L3_gnn_attn).reshape(R, H, 2, HD).transpose(2, 0, 1, 3)
    w3 = np.asarray(L3_gnn_W).transpose(1, 0, 2).reshape(D, R * D)
    arrays = [
        padded(x, P * j, 0).reshape(P, j * D), by_partition(src, pad_node), by_partition(dst, pad_node),
        by_partition(edge_type_4, 0), by_partition(edge_weight, 0), tile_src,
        np.ascontiguousarray(tile_src.reshape(tiles, P).T), np.asarray(edge_attr_256),
        np.asarray(L0_gnn_W), on_all(L0_gnn_b), np.asarray(L2_gnn_W_self), np.asarray(L2_gnn_W_nb),
        on_all(L2_gnn_b_self), on_all(L2_gnn_b_nb), on_all(L2_gnn_gamma), on_all(L2_gnn_beta),
        np.ascontiguousarray(w3), on_all(np.ascontiguousarray(attn)),
    ]
    return n, [np.ascontiguousarray(a) for a in arrays]


def kernel(**inputs):
    from concourse import bacc
    from concourse.bass_utils import run_bass_kernel_spmd

    n, arrays = lay_out(**inputs)
    nc = bacc.Bacc("TRN2", target_bir_lowering=False, num_devices=1)
    given = {f"in_{name}": a for name, a in zip(_INS, arrays)}
    args = [nc.dram_tensor(name, a.shape, mybir.dt.from_np(a.dtype), kind="ExternalInput").ap()
            for name, a in given.items()]
    args.append(nc.dram_tensor("out_x", (n, D), mybir.dt.float32, kind="ExternalOutput").ap())
    build_gnn(nc, *args)
    return run_bass_kernel_spmd(nc, [given], core_ids=[0]).results[0]["out_x"]
```

```python
from contextlib import ExitStack

import concourse.bass as bass
from concourse import mybir

P = 128
D = 128
DE = 256
R = 4
H = 4
HD = D // H
RH = R * H
XW = D + H
G = 10
K = 5
ZERO_PARTS = 8
B = 8
BIG = 1.0e38
LN_EPS = 1e-5
NORM_EPS = 1e-9
SLOPE = 0.2


def steps_per_partition(n_edges):
    return -(-n_edges // (P * 4 * B)) * 4 * B


def node_columns(n_nodes):
    return -(-n_nodes // P)


def chunk_columns(cols):
    return max(c for c in range(1, 9) if cols % (2 * c) == 0)


class Serial:

    def __init__(self, engine, sem):
        self.engine, self.sem, self.base, self.n = engine, sem, 0, 0

    def __call__(self, instruction):
        self.n += 1
        instruction.then_inc(self.sem, 1)
        self.engine.wait_ge(self.sem, self.base + self.n)

    def enter(self, i, per_turn):
        self.start, self.per_turn = self.base + self.n, per_turn
        self.base, self.n = self.start + i * per_turn, 0

    def leave(self, turns):
        assert self.n == self.per_turn, (self.n, self.per_turn)
        self.base, self.n = self.start + turns * self.per_turn, 0


def build_gnn(nc, x_in, src_in, dst_in, type_in, ew_in, tile_src, tile_src_cols, edge_attr,
              w0_in, b0_in, wself_in, wnb_in, bself_in, bnb_in, gamma_in, beta_in, w3_in, attn_in, out):
    f32, i32, bf16 = mybir.dt.float32, mybir.dt.int32, mybir.dt.bfloat16
    ALU = mybir.AluOpType
    ACT = mybir.ActivationFunctionType
    X_AXIS = mybir.AxisListType.X

    J = x_in.shape[1] // D
    NP = P * J
    T = src_in.shape[1]
    EP = P * T
    E = edge_attr.shape[0]
    N = out.shape[0]
    JC = chunk_columns(J)
    NC = J // JC
    PAIRS = E // (2 * G * P)
    U = 2 * PAIRS
    LEFT = E - U * G * P
    NT = (U + 1) * G
    TABLE_ROWS = NP + P
    TURNS = T // (2 * B)
    assert J <= P and 0 < LEFT <= P and T <= NT

    def dram(name, shape, dt=f32):
        return nc.dram_tensor(name, shape, dt, kind="Internal").ap()

    tables = [dram(f"sum_table{k}", (TABLE_ROWS, D)) for k in range(K)]
    h_table = dram("h_table", (NP, D))
    rel_table = dram("rel_table", (NP * R, XW))
    running = dram("running", (EP + P, D))
    rel_edges = dram("rel_edges", (EP, XW))
    adst_nodes = dram("adst_nodes", (NP, RH))
    adst_edges = dram("adst_edges", (EP + NP, RH))
    hi_line = dram("hi_line", (NT * P,), bf16)
    lse_edges = dram("lse_edges", (EP, RH))
    lo_line = dram("lo_line", (NT * P,), bf16)
    deg_line = dram("deg_line", (NP,))
    cum_line = dram("cum_line", (NP,))

    running_steps = running[0:EP, :].rearrange("(p t) d -> p t d", t=T)
    rel_steps = rel_edges.rearrange("(p t) d -> p t d", t=T)
    adst_steps = adst_edges[0:EP, :].rearrange("(p t) c -> p t c", t=T)
    lse_steps = lse_edges.rearrange("(p t) c -> p t c", t=T)
    h_columns = h_table.rearrange("(p j) d -> p j d", j=J)
    rel_columns = rel_table.rearrange("(p j r) d -> p j r d", j=J, r=R)
    adst_columns = adst_nodes.rearrange("(p j) c -> p j c", j=J)
    line = bass.ds

    def after(v):
        return v + 3

    ctx = ExitStack()
    with ctx:
        phase_sems = []

        def sem(name):
            phase_sems.append(nc.alloc_semaphore(name))
            return phase_sems[-1]

        def recycle_semaphores():
            nc.clear_and_free_semaphores(list(phase_sems))
            phase_sems.clear()
            nc.all_engine_barrier()

        def sb(name, shape, dt=f32, scope=ctx):
            return scope.enter_context(nc.sbuf_tensor(name, shape, dt))

        row_bank = ctx.enter_context(nc.psum_tensor("row_bank", [P, 3 * 512], f32))
        bank = [ctx.enter_context(nc.psum_tensor(f"bank{i}", [P, 512], f32)) for i in range(5)]

        x = sb("x", [P, J * D])
        src_idx = sb("src_idx", [P, T], i32)
        rel_idx = sb("rel_idx", [P, T], i32)
        same = sb("same", [P, T + 1])
        is_type = sb("is_type", [P, R, T], bf16)
        ident = sb("ident", [P, P])
        ones = sb("ones", [P, P])
        row_iota = sb("row_iota", [P, P])
        col_iota = sb("col_iota", [P, 1])
        lower = sb("lower", [P, P])
        upper = sb("upper", [P, P])
        from_before = sb("from_before", [P, P])
        from_after = sb("from_after", [P, P])
        bias_before = sb("bias_before", [P, P])
        bias_after = sb("bias_after", [P, P])
        first_end = sb("first_end", [P, 1], i32)
        last_start = sb("last_start", [P, 1], i32)
        first_node = sb("first_node", [P, 1], i32)
        apart = sb("apart", [P, 1])
        ew_prob = sb("ew_prob", [P, T])
        deg = sb("deg", [P, J])
        dinv = sb("dinv", [P, J])
        node_row = sb("node_row", [P, J], i32)
        node_start = sb("node_start", [P, J], i32)
        node_first = sb("node_first", [P, J], i32)
        w0t = sb("w0t", [P, 2, D])
        wself = sb("wself", [P, D])
        wnb = sb("wnb", [P, D])
        gamma = sb("gamma", [P, D])
        beta = sb("beta", [P, D])
        half_bias = sb("half_bias", [P, D])
        w3 = sb("w3", [P, R * D])
        zeros = sb("zeros", [P, TABLE_ROWS // ZERO_PARTS])
        w3_score = sb("w3_score", [P, 2 * RH])
        hist = sb("hist", [P, P])
        passed = sem("passed")
        added = [sem(f"added{k}") for k in range(K)]
        zeros_out = sem("zeros_out")
        dve_own = sem("dve_own")
        own_count = [0]
        phase_sems.clear()

        class Vector(Serial):

            def __init__(self, engine):
                Serial.__init__(self, engine, dve_own)
                self.base = own_count[0]

            def close(self):
                own_count[0] = self.base + self.n

        def columns(c, k):
            return x[:, bass.ds((c * JC + k) * D, D)]

        def chunk(c):
            return x[:, bass.ds(c * JC * D, JC * D)].rearrange("p (j d) -> p j d", d=D)

        class Norm:

            def __init__(self, name, scope):
                self.stats = sb(f"{name}_stats", [P, JC, 6], f32, scope)
                self.mv = sb(f"{name}_mv", [P, JC, 2], f32, scope)
                self.var = sb(f"{name}_var", [P, JC], f32, scope)
                self.std = sb(f"{name}_std", [P, JC], f32, scope)
                self.scale = sb(f"{name}_scale", [P, JC], f32, scope)
                self.shift = sb(f"{name}_shift", [P, JC], f32, scope)
                self.var_ready = sem(f"{name}_var_ready")
                self.std_ready = sem(f"{name}_std_ready")
                self.shift_ready = sem(f"{name}_shift_ready")
                self.out_ready = sem(f"{name}_out_ready")

            OWN = 3

            def vector(self, dve, own, c, col, factor=None):
                dve.sem_inc(passed, 1)
                for k in range(JC):
                    ins = nc.vector.bn_stats(self.stats[:, k, :], col(k))
                own(ins)
                dve.sem_inc(passed, 1)
                for k in range(JC):
                    ins = nc.vector.bn_aggr(self.mv[:, k, :], self.stats[:, k, :])
                own(ins)
                nc.vector.tensor_scalar(self.var[:, :], self.mv[:, :, 1], LN_EPS, None,
                                        ALU.add).then_inc(self.var_ready, 1)
                dve.wait_ge(self.std_ready, c + 1)
                own(nc.vector.reciprocal(self.scale[:, :], self.std[:, :]))
                if factor is not None:
                    own(nc.vector.tensor_tensor(self.scale[:, :], self.scale[:, :], factor, ALU.mult))
                nc.vector.scalar_tensor_tensor(out=self.shift[:, :], in0=self.mv[:, :, 0], scalar=-1.0,
                                               in1=self.scale[:, :], op0=ALU.mult,
                                               op1=ALU.mult).then_inc(self.shift_ready, 1)

            def scalar_std(self, act, c):
                act.wait_ge(self.var_ready, c + 1)
                nc.scalar.activation(self.std[:, :], self.var[:, :], ACT.Sqrt).then_inc(self.std_ready, 1)

            def scalar_apply(self, act, c, col, to, func):
                act.wait_ge(self.shift_ready, c + 1)
                for k in range(JC):
                    ins = nc.scalar.activation(to(k), col(k), func, bias=self.shift[:, k:k + 1],
                                               scale=self.scale[:, k:k + 1])
                ins.then_inc(self.out_ready, 1)

        with ExitStack() as ph:
            dst_i = sb("dst_i", [P, T], i32, ph)
            dstf = sb("dstf", [P, T], f32, ph)
            type_i = sb("type_i", [P, T], i32, ph)
            typef = sb("typef", [P, T], f32, ph)
            srcf = sb("srcf", [P, T], f32, ph)
            ew = sb("ew", [P, T], f32, ph)
            scan_a = sb("scan_a", [P, T], f32, ph)
            scan_b = sb("scan_b", [P, T], f32, ph)
            neg = sb("neg", [P, T + 1], f32, ph)
            w0 = sb("w0", [P, DE], f32, ph)
            b0 = sb("b0", [P, D], f32, ph)
            bself = sb("bself", [P, D], f32, ph)
            bnb = sb("bnb", [P, D], f32, ph)
            attn = sb("attn", [P, 2 * R * D], f32, ph)
            w3a = sb("w3a", [P, R * D], f32, ph)
            diag = sb("diag", [P, 2, P], f32, ph)
            edge_val = sb("edge_val", [P, 8], f32, ph)
            masked = sb("masked", [P, P], f32, ph)
            cnt = sb("cnt", [P, 4], f32, ph)
            first = sb("first", [P, T], bf16, ph)
            last = sb("last", [P, T], bf16, ph)
            h0 = sb("h0", [P, JC, D], f32, ph)
            line_i = sb("line_i", [P, NT], i32, ph)
            line_half = sb("line_half", [P, NT], i32, ph)
            line_bf = sb("line_bf", [P, 2, NT], bf16, ph)

            edges_in = sem("edges_in")
            nodes_in = sem("nodes_in")
            weights_in = sem("weights_in")
            line_in = sem("line_in")
            line_split = sem("line_split")
            lines_out = sem("lines_out")
            iotas = sem("iotas")
            zeros_set = sem("zeros_set")
            diags = sem("diags")
            rows_ready = sem("rows_ready")
            w0_turned = sem("w0_turned")
            max_edges = sem("max_edges")
            max_rows = sem("max_rows")
            ew_shift = sem("ew_shift")
            ew_exp = sem("ew_exp")
            sum_edges = sem("sum_edges")
            sum_carry = sem("sum_carry")
            norm = Norm("norm0", ph)

            block = ph.enter_context(nc.Block("setup"))

            @block.sync
            def _(sp):
                sp.dma_start(dst_i[:, :], dst_in).then_inc(edges_in, 16)
                sp.dma_start(src_idx[:, :], src_in).then_inc(edges_in, 16)
                sp.dma_start(type_i[:, :], type_in).then_inc(edges_in, 16)
                sp.dma_start(ew[:, :], ew_in).then_inc(edges_in, 16)
                sp.dma_start(line_i[:, :], tile_src.rearrange("(p a) -> p a", p=P)).then_inc(line_in, 16)
                sp.dma_start(x[:, :], x_in).then_inc(nodes_in, 16)
                sp.dma_start(b0[:, :], b0_in).then_inc(nodes_in, 16)
                for to, of in ((w0, w0_in), (wself, wself_in), (wnb, wnb_in), (bself, bself_in),
                               (bnb, bnb_in), (gamma, gamma_in), (beta, beta_in), (w3, w3_in),
                               (attn, attn_in)):
                    sp.dma_start(to[:, :], of).then_inc(weights_in, 16)
                sp.wait_ge(line_split, 1)
                sp.dma_start(hi_line.rearrange("(p a) -> p a", p=P), line_bf[:, 0, :]).then_inc(lines_out, 16)
                sp.dma_start(lo_line.rearrange("(p a) -> p a", p=P), line_bf[:, 1, :]).then_inc(lines_out, 16)
                sp.wait_ge(zeros_set, 1)
                sp.dma_start(running[EP:EP + P, :], zeros[:, 0:D]).then_inc(zeros_out, 16)
                sp.wait_ge(zeros_out, 16)
                sp.wait_ge(lines_out, 32)

            @block.gpsimd
            def _(pool):
                nc.gpsimd.iota(row_iota[:, :], [[1, P]], base=0, channel_multiplier=0,
                               allow_small_or_imprecise_dtypes=True).then_inc(iotas, 1)
                nc.gpsimd.iota(col_iota[:, :], [[0, 1]], base=0, channel_multiplier=1,
                               allow_small_or_imprecise_dtypes=True).then_inc(iotas, 1)
                nc.gpsimd.memset(zeros[:, :], 0.0).then_inc(zeros_set, 1)
                pool.wait_ge(zeros_set, 1)
                pool.wait_ge(edges_in, 64)
                pool.wait_ge(weights_in, 16 * 9)
                pool.wait_ge(nodes_in, 32)
                width = TABLE_ROWS // ZERO_PARTS
                for k in range(K):
                    nc.gpsimd.dma_start(
                        tables[k].rearrange("(p a) d -> p (a d)", p=P).rearrange("p (k w) -> p k w", w=width),
                        zeros[:, :].unsqueeze(1).broadcast_to([P, ZERO_PARTS, width])).then_inc(added[k], 16)

            @block.vector
            def _(dve):
                own = Vector(dve)
                dve.wait_ge(line_in, 16)
                own(nc.vector.tensor_scalar(line_half[:, :], line_i[:, :], 7, None, ALU.logical_shift_right))
                own(nc.vector.tensor_copy(line_bf[:, 0, :], line_half[:, :]))
                own(nc.vector.tensor_scalar(line_half[:, :], line_i[:, :], 127, None, ALU.bitwise_and))
                nc.vector.tensor_copy(line_bf[:, 1, :], line_half[:, :]).then_inc(line_split, 1)

                dve.wait_ge(iotas, 2)
                nc.vector.tensor_scalar(ident[:, :], row_iota[:, :], col_iota[:, :], None, ALU.is_equal)
                nc.vector.tensor_scalar(lower[:, :], row_iota[:, :], col_iota[:, :], None, ALU.is_lt)
                nc.vector.tensor_scalar(upper[:, :], row_iota[:, :], col_iota[:, :], None, ALU.is_gt)
                nc.vector.memset(ones[:, :], 1.0)
                own(nc.vector.memset(hist[:, :], 0.0))

                dve.wait_ge(edges_in, 64)
                nc.vector.memset(same[:, 0:1], 0.0)
                nc.vector.memset(same[:, T:T + 1], 0.0)
                nc.vector.tensor_copy(first_node[:, :], dst_i[:, 0:1])
                nc.vector.tensor_copy(srcf[:, :], src_idx[:, :])
                nc.vector.tensor_copy(typef[:, :], type_i[:, :])
                own(nc.vector.tensor_copy(dstf[:, :], dst_i[:, :]))
                nc.vector.tensor_tensor(same[:, 1:T], dstf[:, 1:T], dstf[:, 0:T - 1], ALU.is_equal)
                nc.vector.tensor_scalar(first[:, :], dstf[:, :], dstf[:, 0:1], None, ALU.is_equal)
                nc.vector.tensor_scalar(last[:, :], dstf[:, :], dstf[:, T - 1:T], None, ALU.is_equal)
                for r in range(R):
                    nc.vector.tensor_scalar(is_type[:, r, :], typef[:, :], float(r), None, ALU.is_equal)
                nc.vector.scalar_tensor_tensor(out=rel_idx[:, :], in0=srcf[:, :], scalar=float(R),
                                               in1=typef[:, :], op0=ALU.mult, op1=ALU.add)
                nc.vector.tensor_scalar(diag[:, 0, :], ident[:, :], dstf[:, 0:1], None, ALU.mult)
                nc.vector.tensor_scalar(diag[:, 1, :], ident[:, :], dstf[:, T - 1:T], None,
                                        ALU.mult).then_inc(diags, 1)
                dve.wait_ge(diags, 1)
                own(nc.vector.tensor_scalar(neg[:, :], same[:, :], -1.0, BIG, ALU.add, ALU.mult))
                own(nc.vector.reduce_sum(cnt[:, 0:1], first[:, :], X_AXIS))
                own(nc.vector.tensor_scalar(cnt[:, 1:2], col_iota[:, :], float(T), -1.0, ALU.mult, ALU.add))
                own(nc.vector.tensor_tensor(first_end[:, :], cnt[:, 0:1], cnt[:, 1:2], ALU.add))
                own(nc.vector.reduce_sum(cnt[:, 2:3], last[:, :], X_AXIS))
                own(nc.vector.tensor_scalar(cnt[:, 3:4], col_iota[:, :], float(T), float(T), ALU.mult, ALU.add))
                own(nc.vector.tensor_tensor(last_start[:, :], cnt[:, 3:4], cnt[:, 2:3], ALU.subtract))
                own(nc.vector.tensor_tensor(apart[:, :], dstf[:, 0:1], dstf[:, T - 1:T], ALU.is_equal))
                own(nc.vector.tensor_scalar(apart[:, :], apart[:, :], -1.0, BIG, ALU.add, ALU.mult))
                dve.wait_ge(rows_ready, 1)
                nc.vector.scalar_tensor_tensor(out=from_before[:, :], in0=bank[0][:, 0:P],
                                               scalar=dstf[:, T - 1:T], in1=upper[:, :],
                                               op0=ALU.is_equal, op1=ALU.mult)
                own(nc.vector.scalar_tensor_tensor(out=from_after[:, :], in0=bank[1][:, 0:P],
                                                   scalar=dstf[:, 0:1], in1=lower[:, :],
                                                   op0=ALU.is_equal, op1=ALU.mult))
                nc.vector.tensor_scalar(bias_before[:, :], from_after[:, :], -1.0, BIG, ALU.add, ALU.mult)
                own(nc.vector.tensor_scalar(bias_after[:, :], from_before[:, :], -1.0, BIG, ALU.add, ALU.mult))

                own(nc.vector.tensor_tensor_scan(scan_a[:, :], neg[:, 0:T], ew[:, :], 0.0, ALU.add, ALU.max))
                own(nc.vector.tensor_tensor_scan(scan_b[:, ::-1], neg[:, 1:T + 1][:, ::-1],
                                                 scan_a[:, ::-1], 0.0, ALU.add, ALU.max))
                nc.vector.tensor_scalar(diag[:, 0, :], ident[:, :], scan_a[:, T - 1:T], None, ALU.mult)
                nc.vector.tensor_scalar(diag[:, 1, :], ident[:, :], scan_b[:, 0:1], None,
                                        ALU.mult).then_inc(max_edges, 1)
                dve.wait_ge(max_rows, 1)
                own(nc.vector.tensor_tensor(masked[:, :], bank[0][:, 0:P], bias_before[:, :], ALU.add))
                own(nc.vector.tensor_reduce(edge_val[:, 0:1], masked[:, :], X_AXIS, ALU.max))
                own(nc.vector.tensor_tensor(masked[:, :], bank[1][:, 0:P], bias_after[:, :], ALU.add))
                own(nc.vector.tensor_reduce(edge_val[:, 1:2], masked[:, :], X_AXIS, ALU.max))
                for mask, k in ((first, 0), (last, 1)):
                    own(nc.vector.tensor_scalar(scan_a[:, :], mask[:, :], -1.0, BIG, ALU.add, ALU.mult))
                    own(nc.vector.scalar_tensor_tensor(out=scan_b[:, :], in0=scan_a[:, :],
                                                       scalar=edge_val[:, k:k + 1], in1=scan_b[:, :],
                                                       op0=ALU.add, op1=ALU.max))
                nc.vector.tensor_tensor(scan_a[:, :], ew[:, :], scan_b[:, :], ALU.subtract).then_inc(ew_shift, 1)
                dve.wait_ge(ew_exp, 1)
                own(nc.vector.tensor_tensor_scan(scan_a[:, :], same[:, 0:T], ew[:, :], 0.0, ALU.mult, ALU.add))
                own(nc.vector.tensor_copy(edge_val[:, 2:3], scan_a[:, T - 1:T]))
                own(nc.vector.scalar_tensor_tensor(out=scan_b[:, :], in0=same[:, 1:T + 1], scalar=1.0,
                                                   in1=scan_a[:, :], op0=ALU.is_lt, op1=ALU.mult))
                own(nc.vector.tensor_tensor_scan(scan_a[:, ::-1], same[:, 1:T + 1][:, ::-1],
                                                 scan_b[:, ::-1], 0.0, ALU.mult, ALU.add))
                nc.vector.tensor_copy(edge_val[:, 3:4], scan_a[:, 0:1]).then_inc(sum_edges, 1)
                dve.wait_ge(sum_carry, 1)
                own(nc.vector.tensor_copy(edge_val[:, 4:6], bank[2][:, 0:2]))
                own(nc.vector.scalar_tensor_tensor(out=scan_b[:, :], in0=first[:, :], scalar=edge_val[:, 4:5],
                                                   in1=scan_a[:, :], op0=ALU.mult, op1=ALU.add))
                own(nc.vector.scalar_tensor_tensor(out=scan_a[:, :], in0=last[:, :], scalar=edge_val[:, 5:6],
                                                   in1=scan_b[:, :], op0=ALU.mult, op1=ALU.add))
                own(nc.vector.reciprocal(scan_b[:, :], scan_a[:, :]))
                own(nc.vector.tensor_tensor(ew_prob[:, :], ew[:, :], scan_b[:, :], ALU.mult))

                dve.wait_ge(weights_in, 16 * 9)
                dve.wait_ge(w0_turned, 1)
                nc.vector.tensor_copy(w0t[:, :, :].rearrange("p c d -> p (c d)"), bank[3][:, 0:2 * D])
                own(nc.vector.tensor_tensor(half_bias[:, :], bself[:, :], bnb[:, :], ALU.add))
                own(nc.vector.tensor_scalar(half_bias[:, :], half_bias[:, :], 0.5, None, ALU.mult))
                for side in range(2):
                    own(nc.vector.tensor_tensor(w3a[:, :], w3[:, :], attn[:, side * R * D:(side + 1) * R * D],
                                                ALU.mult))
                    own(nc.vector.reduce_sum(w3_score[:, side * RH:(side + 1) * RH],
                                             w3a[:, :].rearrange("p (c d) -> p c d", d=HD), X_AXIS))

                dve.wait_ge(nodes_in, 32)
                with dve.Fori(0, NC) as c:
                    own.enter(c, Norm.OWN + 2)
                    norm.vector(dve, own, c, lambda k: columns(c, k))
                    dve.wait_ge(norm.out_ready, c + 1)
                    own(nc.vector.tensor_tensor(chunk(c), chunk(c), h0[:, :, :], ALU.add))
                    own(nc.vector.tensor_tensor(chunk(c), chunk(c),
                                                b0[:, :].unsqueeze(1).broadcast_to([P, JC, D]), ALU.add))
                own.leave(NC)
                own.close()

            @block.scalar
            def _(act):
                act.wait_ge(ew_shift, 1)
                nc.scalar.activation(ew[:, :], scan_a[:, :], ACT.Exp).then_inc(ew_exp, 1)
                act.wait_ge(nodes_in, 32)
                with act.Fori(0, NC) as c:
                    norm.scalar_std(act, c)
                    norm.scalar_apply(act, c, lambda k: columns(c, k), lambda k: h0[:, k, :], ACT.Relu)

            @block.tensor
            def _(pe):
                pe.wait_ge(diags, 1)
                for k in range(2):
                    ins = nc.tensor.matmul(bank[k][:, 0:P], ones[:, :], diag[:, k, :], start=True, stop=True)
                ins.then_inc(rows_ready, 1)
                pe.wait_ge(weights_in, 16 * 9)
                for c in range(2):
                    ins = nc.tensor.transpose(bank[3][:, c * D:(c + 1) * D], w0[:, c * D:(c + 1) * D], ident[:, :])
                ins.then_inc(w0_turned, 1)
                pe.wait_ge(max_edges, 1)
                for k in range(2):
                    ins = nc.tensor.matmul(bank[k][:, 0:P], ones[:, :], diag[:, k, :], start=True, stop=True)
                ins.then_inc(max_rows, 1)
                pe.wait_ge(sum_edges, 1)
                nc.tensor.matmul(bank[2][:, 0:1], from_before[:, :], edge_val[:, 2:3], start=True, stop=True)
                nc.tensor.matmul(bank[2][:, 1:2], from_after[:, :], edge_val[:, 3:4], start=True,
                                 stop=True).then_inc(sum_carry, 1)

        with ExitStack() as ph:
            attrs = sb("attrs", [P, 2, G, DE], f32, ph)
            rows = sb("rows", [2, 2, G * P], bf16, ph)
            halves = sb("halves", [2, P], bf16, ph)
            cols = sb("cols", [P, NT], f32, ph)
            away = sb("away", [P, NT], f32, ph)
            high = sb("high", [P, NT], bf16, ph)
            low = sb("low", [P, NT], bf16, ph)
            iota_bf = sb("iota_bf", [P, P], bf16, ph)
            equal = sb("equal", [P, 2, G, P], f32, ph)
            earlier = sb("earlier", [P, G, P], f32, ph)
            n_earlier = sb("n_earlier", [P, G], f32, ph)
            move = sb("move", [P, G], f32, ph)
            add_idx = sb("add_idx", [P, 2, G], i32, ph)
            hot_high = sb("hot_high", [P, 2, G, J], bf16, ph)
            hot_low = sb("hot_low", [P, 2, G, P], bf16, ph)
            pair_sum = sb("pair_sum", [P, 2, 4 * P], f32, ph)
            project = sb("project", [P, 2, G, D], f32, ph)
            own_row = sb("own_row", [P, 1], f32, ph)
            cols_i = project[:, :, :, :].rearrange("p a b d -> p (a b d)")[:, 0:NT].bitcast(i32)
            dst_half = project[:, :, :, :].rearrange("p a b d -> p (a b d)")[:, 0:T].bitcast(i32)
            dst_i2 = equal[:, :, :, :].rearrange("p a b d -> p (a b d)")[:, 0:T].bitcast(i32)

            cols_in = sem("cols_in")
            consts = sem("consts")
            attrs_in = [sem(f"attrs_in{h}") for h in range(2)]
            rows_in = [sem(f"rows_in{h}") for h in range(2)]
            tail_clear = sem("tail_clear")
            rows_spread = sem("rows_spread")
            equal_ready = sem("equal_ready")
            idx_ready = sem("idx_ready")
            hots_ready = sem("hots_ready")
            group_done = sem("group_done")
            hist_taken = sem("hist_taken")
            pair_made = sem("pair_made")
            pair_copied = sem("pair_copied")
            pair_projected = sem("pair_projected")
            project_copied = sem("project_copied")
            adds_landed = sem("adds_landed")
            spare_rows_hit = G // K
            NPAIR = G // 2

            block = ph.enter_context(nc.Block("layer0"))

            def wait_added(engine, u):
                engine.wait_ge(adds_landed, after(u - 2))

            @block.sync
            def _(sp):
                sp.dma_start(cols_i, tile_src_cols).then_inc(cols_in, 16)
                sp.dma_start(dst_i2, dst_in).then_inc(cols_in, 16)

                def load(u, h):
                    sp.wait_ge(rows_spread, after(u - 2))
                    for part, of in enumerate((hi_line, lo_line)):
                        sp.dma_start(rows[part:part + 1, h, :],
                                     of[line(u * G * P, G * P)].rearrange("(a n) -> a n", a=1)
                                     ).then_inc(rows_in[h], 16)

                groups = edge_attr[0:U * G * P, :].rearrange("(u p b) f -> u p (b f)", p=P, b=G)
                with sp.Fori(0, PAIRS) as i:
                    for h in range(2):
                        u = 2 * i + h
                        load(u, h)
                        sp.wait_ge(group_done, after(u - 2))
                        sp.dma_start(attrs[:, h, :, :].rearrange("p b f -> p (b f)"),
                                     groups[line(u, 1), :, :].rearrange("u p f -> (u p) f")
                                     ).then_inc(attrs_in[h], 16)
                load(U, 0)
                sp.wait_ge(tail_clear, 1)
                sp.dma_start(attrs[0:LEFT, 0, 0, :], edge_attr[U * G * P:E, :]).then_inc(attrs_in[0], 16)

            @block.gpsimd
            def _(pool):
                pool.sem_inc(adds_landed, 1)

                def add_group(u, h, tiles):
                    pool.wait_ge(idx_ready, after(u))
                    for b in range(tiles):
                        k = b % K
                        if b % 2 == 0:
                            pool.wait_ge(project_copied, after(u * NPAIR + b // 2))
                        pool.wait_ge(added[k], 16 * (spare_rows_hit * u + b // K + 1))
                        pool.sem_inc(adds_landed if b == K else passed, 1)
                        nc.gpsimd.indirect_dma_start(
                            tables[k], bass.IndirectOffsetOnAxis(ap=add_idx[:, h, b:b + 1], axis=0),
                            project[:, h, b, :], None, compute_op=ALU.add).then_inc(added[k], 16)

                with pool.Fori(0, PAIRS) as i:
                    for h in range(2):
                        add_group(2 * i + h, h, G)
                add_group(U, 0, 1)
                for k in range(K):
                    pool.wait_ge(added[k], 16 * (spare_rows_hit * U + 1 + (k == 0)))

            @block.vector
            def _(dve):
                own = Vector(dve)
                for s in (equal_ready, idx_ready, hots_ready, hist_taken):
                    dve.sem_inc(s, 2)
                nc.vector.memset(halves[0:2, :], 1.0)
                nc.vector.memset(bank[4][:, 0:P], 0.0)
                own(nc.vector.tensor_copy(iota_bf[:, :], row_iota[:, :]))
                nc.vector.memset(halves[0:1, :], 128.0).then_inc(consts, 1)
                nc.vector.tensor_scalar(own_row[:, :], col_iota[:, :], float(NP), None, ALU.add)
                nc.vector.memset(high[:, :], 255.0)
                own(nc.vector.memset(low[:, :], 255.0))
                dve.wait_ge(cols_in, 32)
                own(nc.vector.tensor_copy(cols[:, :], cols_i))
                nc.vector.tensor_scalar(away[:, :], cols[:, :], -1.0, own_row[:, :], ALU.mult, ALU.add)
                own(nc.vector.tensor_scalar(dst_half, dst_i2, 7, None, ALU.logical_shift_right))
                own(nc.vector.tensor_copy(high[:, 0:T], dst_half))
                own(nc.vector.tensor_scalar(dst_half, dst_i2, 127, None, ALU.bitwise_and))
                own(nc.vector.tensor_copy(low[:, 0:T], dst_half))

                def take_hist(u):
                    dve.wait_ge(group_done, after(u))
                    nc.vector.tensor_tensor(hist[0:J, :], hist[0:J, :], bank[4][0:J, 0:P],
                                            ALU.add).then_inc(hist_taken, 1)

                def group(u, h):
                    here = line(u * G, G)
                    dve.wait_ge(rows_spread, after(u))
                    dve.wait_ge(group_done, after(u - 2))
                    nc.vector.tensor_tensor(
                        equal[:, h, :, :], row_bank[:, 0:G * P].rearrange("p (b q) -> p b q", q=P),
                        cols[:, here].unsqueeze(2).broadcast_to([P, G, P]), ALU.is_equal).then_inc(equal_ready, 1)
                    dve.wait_ge(equal_ready, after(u))
                    own(nc.vector.tensor_tensor(earlier[:, :, :], equal[:, h, :, :],
                                                lower[:, :].unsqueeze(1).broadcast_to([P, G, P]), ALU.mult))
                    own(nc.vector.reduce_sum(n_earlier[:, :], earlier[:, :, :], X_AXIS))
                    own(nc.vector.scalar_tensor_tensor(out=move[:, :], in0=n_earlier[:, :], scalar=0.0,
                                                       in1=away[:, here], op0=ALU.is_gt, op1=ALU.mult))
                    wait_added(dve, u)
                    nc.vector.tensor_tensor(add_idx[:, h, :], move[:, :], cols[:, here],
                                            ALU.add).then_inc(idx_ready, 1)
                    dve.wait_ge(group_done, after(u - 2))
                    nc.vector.tensor_tensor(hot_high[:, h, :, :],
                                            iota_bf[:, 0:J].unsqueeze(1).broadcast_to([P, G, J]),
                                            high[:, here].unsqueeze(2).broadcast_to([P, G, J]), ALU.is_equal)
                    nc.vector.tensor_tensor(hot_low[:, h, :, :],
                                            iota_bf[:, :].unsqueeze(1).broadcast_to([P, G, P]),
                                            low[:, here].unsqueeze(2).broadcast_to([P, G, P]),
                                            ALU.is_equal).then_inc(hots_ready, 1)
                    take_hist(u - 1)

                with dve.Fori(0, PAIRS) as i:
                    own.enter(i, 6)
                    for h in range(2):
                        group(2 * i + h, h)
                own.leave(PAIRS)
                dve.wait_ge(group_done, after(U - 2))
                nc.vector.memset(attrs[:, 0, 0, :], 0.0).then_inc(tail_clear, 1)
                group(U, 0)
                take_hist(U)
                own.close()

            @block.scalar
            def _(act):
                act.sem_inc(pair_copied, 2)
                act.sem_inc(project_copied, 2)

                def copy_pair(q, par, n):
                    act.wait_ge(pair_made, after(q))
                    act.wait_ge(pair_projected, after(q - 2))
                    nc.scalar.copy(pair_sum[:, par, 0:n * 2 * P], bank[par][:, 0:n * 2 * P]).then_inc(pair_copied, 1)

                def copy_project(q, par, h, k, n):
                    act.wait_ge(pair_projected, after(q))
                    nc.scalar.copy(project[:, h, 2 * k:2 * k + n, :].rearrange("p b d -> p (b d)"),
                                   bank[2 + par][:, 0:n * D]).then_inc(project_copied, 1)

                with act.Fori(0, PAIRS) as i:
                    for h in range(2):
                        u = 2 * i + h
                        for k in range(NPAIR):
                            copy_pair(u * NPAIR + k, (h * NPAIR + k) % 2, 2)
                            if k == 1:
                                wait_added(act, u)
                            if k:
                                copy_project(u * NPAIR + k - 1, (h * NPAIR + k - 1) % 2, h, k - 1, 2)
                        copy_project(u * NPAIR + NPAIR - 1, (h * NPAIR + NPAIR - 1) % 2, h, NPAIR - 1, 2)
                copy_pair(U * NPAIR, 0, 1)
                wait_added(act, U)
                copy_project(U * NPAIR, 0, 0, 0, 1)

            @block.tensor
            def _(pe):
                for s in (rows_spread, group_done, pair_made, pair_projected):
                    pe.sem_inc(s, 2)
                pe.wait_ge(consts, 1)

                def spread_rows(u, h, turn):
                    pe.wait_ge(rows_in[h], 32 * (turn + 1))
                    pe.wait_ge(equal_ready, after(u - 1))
                    for at in range(0, G * P, 512):
                        n = min(512, G * P - at)
                        ins = nc.tensor.matmul(row_bank[:, at:at + n], halves[0:2, :], rows[0:2, h, at:at + n],
                                               start=True, stop=True)
                    ins.then_inc(rows_spread, 1)

                def sum_pair(q, par, h, k, n):
                    pe.wait_ge(pair_copied, after(q - 2))
                    for t in range(n):
                        for c in range(2):
                            at = (2 * t + c) * P
                            ins = nc.tensor.matmul(bank[par][:, at:at + P],
                                                   attrs[:, h, 2 * k + t, c * P:(c + 1) * P],
                                                   equal[:, h, 2 * k + t, :], start=True, stop=True)
                    ins.then_inc(pair_made, 1)

                def project_pair(q, par, n):
                    pe.wait_ge(pair_copied, after(q))
                    pe.wait_ge(project_copied, after(q - 2))
                    for t in range(n):
                        for c in range(2):
                            at = (2 * t + c) * P
                            ins = nc.tensor.matmul(bank[2 + par][:, t * D:(t + 1) * D],
                                                   pair_sum[:, par, at:at + P], w0t[:, c, :],
                                                   start=(c == 0), stop=(c == 1))
                    ins.then_inc(pair_projected, 1)

                def add_hist(u, h):
                    pe.wait_ge(hots_ready, after(u))
                    pe.wait_ge(hist_taken, after(u))
                    for b in range(G):
                        ins = nc.tensor.matmul(bank[4][0:J, 0:P], hot_high[:, h, b, :], hot_low[:, h, b, :],
                                               start=(b == 0), stop=(b == G - 1))
                    ins.then_inc(group_done, 1)

                spread_rows(0, 0, 0)
                with pe.Fori(0, PAIRS) as i:
                    for h in range(2):
                        u = 2 * i + h
                        pe.wait_ge(attrs_in[h], 16 * (i + 1))
                        pe.wait_ge(equal_ready, after(u))
                        for k in range(NPAIR):
                            sum_pair(u * NPAIR + k, (h * NPAIR + k) % 2, h, k, 2)
                            if k == 0:
                                spread_rows(u + 1, 1 - h, i + h)
                            if k:
                                project_pair(u * NPAIR + k - 1, (h * NPAIR + k - 1) % 2, 2)
                        add_hist(u, h)
                        project_pair(u * NPAIR + NPAIR - 1, (h * NPAIR + NPAIR - 1) % 2, 2)
                pe.wait_ge(attrs_in[0], 16 * (PAIRS + 1))
                pe.wait_ge(equal_ready, after(U))
                sum_pair(U * NPAIR, 0, 0, 0, 1)
                add_hist(U, 0)
                project_pair(U * NPAIR, 0, 1)

        recycle_semaphores()

        class Gather:

            def __init__(self, name, scope, width, used):
                self.rows = sb(f"{name}_rows", [P, 2, B, width], f32, scope)
                self.stage = sb(f"{name}_stage", [P, 2, B], i32, scope)
                self.staged = sem(f"{name}_staged")
                self.got = [sem(f"{name}_got{h}") for h in range(2)]
                self.used = used

            def pool(self, pool, table):
                with pool.Fori(0, TURNS) as i:
                    for h in range(2):
                        u = 2 * i + h
                        pool.wait_ge(self.staged, after(u))
                        pool.wait_ge(self.used, after(u - 2))
                        pool.sem_inc(passed, 1)
                        for b in range(B):
                            nc.gpsimd.indirect_dma_start(
                                self.rows[:, h, b, :], None, table,
                                bass.IndirectOffsetOnAxis(ap=self.stage[:, h, b:b + 1], axis=0)
                                ).then_inc(self.got[h], 16)

            def scalar_stage(self, act, idx, u, h):
                act.wait_ge(self.used, after(u - 2))
                nc.scalar.copy(self.stage[:, h, :], idx[:, line(u * B, B)]).then_inc(self.staged, 1)

            def wait_rows(self, engine, i, h):
                engine.wait_ge(self.got[h], 16 * B * (i + 1))

        class RunningSums:

            def __init__(self, name, scope):
                self.sums = sb(f"{name}_sums", [P, 2, B, D], f32, scope)
                self.carry = sb(f"{name}_carry", [P, D], f32, scope)
                self.summed = sem(f"{name}_summed")
                self.stored = [sem(f"{name}_stored{h}") for h in range(2)]
                self.carried = sem(f"{name}_carried")
                self.carry_copied = sem(f"{name}_carry_copied")
                self.whole = sem(f"{name}_whole")

            OWN = B - 1

            def vector_start(self, dve, own):
                dve.sem_inc(self.summed, 2)
                own(nc.vector.memset(self.sums[:, 1, :, :], 0.0))

            def vector(self, dve, own, i, h, rows):
                u = 2 * i + h
                dve.wait_ge(self.stored[h], 16 * (i + 1))
                dve.wait_ge(self.summed, after(u - 1))
                for b in range(B):
                    before = self.sums[:, h, b - 1, :] if b else self.sums[:, 1 - h, B - 1, :]
                    ins = nc.vector.scalar_tensor_tensor(
                        out=self.sums[:, h, b, :], in0=before, scalar=same[:, line(u * B + b, 1)],
                        in1=rows(b), op0=ALU.mult, op1=ALU.add)
                    if b < B - 1:
                        own(ins)
                ins.then_inc(self.summed, 1)

            def sync_start(self, sp):
                for h in range(2):
                    sp.sem_inc(self.stored[h], 16)

            def sync(self, sp, i, h):
                u = 2 * i + h
                sp.wait_ge(self.summed, after(u))
                sp.dma_start(running_steps[:, line(u * B, B), :], self.sums[:, h, :, :]).then_inc(self.stored[h], 16)

            def tensor_carry(self, pe, sharing, ends):
                pe.wait_ge(self.summed, after(2 * TURNS - 1))
                nc.tensor.matmul(bank[0][:, 0:D], sharing[:, :], ends,
                                 start=True, stop=True).then_inc(self.carried, 1)

            def vector_carry(self, dve):
                dve.wait_ge(self.carried, 1)
                nc.vector.tensor_copy(self.carry[:, :], bank[0][:, 0:D]).then_inc(self.carry_copied, 1)

            def pool_carry(self, pool, row):
                for h in range(2):
                    pool.wait_ge(self.stored[h], 16 * (TURNS + 1))
                pool.wait_ge(self.carry_copied, 1)
                nc.gpsimd.indirect_dma_start(
                    running, bass.IndirectOffsetOnAxis(ap=row[:, :], axis=0),
                    self.carry[:, :], None, compute_op=ALU.add).then_inc(self.whole, 16)

        class NodeSums:

            def __init__(self, name, scope, row_of_node):
                self.row_of_node = row_of_node
                self.rows = sb(f"{name}_rows", [P, 2, JC, D], f32, scope)
                self.stage = sb(f"{name}_stage", [P, 2, JC], i32, scope)
                self.staged = sem(f"{name}_staged")
                self.got = [sem(f"{name}_got{h}") for h in range(2)]
                self.used = sem(f"{name}_used")

            def pool(self, pool, whole):
                with pool.Fori(0, NC // 2) as i:
                    for h in range(2):
                        c = 2 * i + h
                        pool.wait_ge(self.staged, after(c))
                        pool.wait_ge(self.used, after(c - 2))
                        pool.wait_ge(whole, 16)
                        pool.sem_inc(passed, 1)
                        for k in range(JC):
                            nc.gpsimd.indirect_dma_start(
                                self.rows[:, h, k, :], None, running,
                                bass.IndirectOffsetOnAxis(ap=self.stage[:, h, k:k + 1], axis=0)
                                ).then_inc(self.got[h], 16)

            def scalar_stage(self, act, c, h):
                act.wait_ge(self.used, after(c - 2))
                nc.scalar.copy(self.stage[:, h, :], self.row_of_node[:, line(c * JC, JC)]).then_inc(self.staged, 1)

            def wait_rows(self, engine, i, h):
                engine.wait_ge(self.got[h], 16 * JC * (i + 1))

        with ExitStack() as ph:
            part = sb("part", [P, 2, K, JC * D], f32, ph)
            hout = sb("hout", [P, 2, JC, D], f32, ph)
            line_cum = sb("line_cum", [P, P], f32, ph)
            hist_sum = sb("hist_sum", [P, 1], f32, ph)
            hist_off = sb("hist_off", [P, 1], f32, ph)
            cum = sb("cum", [P, J], f32, ph)
            has = sb("has", [P, J], f32, ph)
            has_row = sb("has_row", [P, 1], f32, ph)
            tmp = sb("tmp", [P, J], f32, ph)
            tmp2 = sb("tmp2", [P, J], f32, ph)
            dump = sb("dump", [P, J], f32, ph)
            hist_summed = sem("hist_summed")
            hist_offset = sem("hist_offset")
            cum_ready = sem("cum_ready")
            lines_stored = sem("lines_stored")
            lines_loaded = sem("lines_loaded")
            deg_floor = sem("deg_floor")
            deg_root = sem("deg_root")
            parts_in = [sem(f"parts_in{h}") for h in range(2)]
            parts_used = sem("parts_used")
            h_stored = [sem(f"h1_stored{h}") for h in range(2)]
            norm = Norm("norm1", ph)
            block = ph.enter_context(nc.Block("nodes1"))

            @block.sync
            def _(sp):
                for h in range(2):
                    sp.sem_inc(h_stored[h], 16)
                sp.wait_ge(cum_ready, 1)
                sp.dma_start(deg_line.rearrange("(a b) -> a b", b=P), hist[0:J, :]).then_inc(lines_stored, 16)
                sp.dma_start(cum_line.rearrange("(a b) -> a b", b=P), line_cum[0:J, :]).then_inc(lines_stored, 16)
                sp.wait_ge(lines_stored, 32)
                sp.dma_start(deg[:, :], deg_line.rearrange("(p j) -> p j", p=P)).then_inc(lines_loaded, 16)
                sp.dma_start(cum[:, :], cum_line.rearrange("(p j) -> p j", p=P)).then_inc(lines_loaded, 16)

                def load(c, h):
                    sp.wait_ge(parts_used, after(c - 2))
                    for k in range(K):
                        view = tables[k][0:NP, :].rearrange("(p j) d -> p (j d)", p=P)
                        sp.dma_start(part[:, h, k, :], view[:, line(c * JC * D, JC * D)]).then_inc(parts_in[h], 16)

                def store(i, h):
                    sp.wait_ge(norm.out_ready, 2 * i + h + 1)
                    sp.dma_start(h_columns[:, line((2 * i + h) * JC, JC), :], hout[:, h, :, :]
                                 ).then_inc(h_stored[h], 16)

                with sp.Fori(0, NC // 2) as i:
                    for h in range(2):
                        load(2 * i + h, h)
                    for h in range(2):
                        store(i, h)
                for h in range(2):
                    sp.wait_ge(h_stored[h], 16 * (NC // 2 + 1))

            @block.vector
            def _(dve):
                own = Vector(dve)
                dve.sem_inc(parts_used, 2)
                own(nc.vector.reduce_sum(hist_sum[:, :], hist[:, :], X_AXIS))
                nc.vector.tensor_tensor_scan(line_cum[:, :], ones[:, :], hist[:, :], 0.0, ALU.mult,
                                             ALU.add).then_inc(hist_summed, 1)
                dve.wait_ge(hist_summed, 1)
                dve.wait_ge(hist_offset, 1)
                own(nc.vector.tensor_copy(hist_off[:, :], bank[0][:, 0:1]))
                nc.vector.tensor_scalar(line_cum[:, :], line_cum[:, :], hist_off[:, :], None,
                                        ALU.add).then_inc(cum_ready, 1)
                dve.wait_ge(lines_loaded, 32)
                own(nc.vector.tensor_scalar(has[:, :], deg[:, :], 0.0, None, ALU.is_gt))
                nc.vector.tensor_scalar(tmp[:, :], deg[:, :], 1.0, None, ALU.max).then_inc(deg_floor, 1)
                dve.wait_ge(deg_root, 1)
                own(nc.vector.reciprocal(tmp[:, :], tmp2[:, :]))
                own(nc.vector.tensor_tensor(dinv[:, :], tmp[:, :], has[:, :], ALU.mult))
                own(nc.vector.tensor_scalar(tmp[:, :], cum[:, :], -1.0 - EP, None, ALU.add))
                own(nc.vector.tensor_tensor(tmp[:, :], tmp[:, :], has[:, :], ALU.mult))
                own(nc.vector.tensor_scalar(node_row[:, :], tmp[:, :], float(EP), None, ALU.add))
                own(nc.vector.tensor_scalar(has_row[:, :], col_iota[:, :], float(J), float(EP), ALU.mult, ALU.add))
                own(nc.vector.tensor_scalar(dump[:, :], row_iota[:, 0:J], has_row[:, :], None, ALU.add))
                own(nc.vector.tensor_tensor(tmp[:, :], cum[:, :], deg[:, :], ALU.subtract))
                own(nc.vector.tensor_scalar(tmp2[:, :], tmp[:, :], float(EP), None, ALU.subtract))
                own(nc.vector.tensor_tensor(tmp2[:, :], tmp2[:, :], has[:, :], ALU.mult))
                own(nc.vector.tensor_scalar(node_first[:, :], tmp2[:, :], float(EP), None, ALU.add))
                own(nc.vector.tensor_tensor(tmp[:, :], tmp[:, :], dump[:, :], ALU.subtract))
                own(nc.vector.tensor_tensor(tmp[:, :], tmp[:, :], has[:, :], ALU.mult))
                own(nc.vector.tensor_tensor(node_start[:, :], tmp[:, :], dump[:, :], ALU.add))
                with dve.Fori(0, NC // 2) as i:
                    own.enter(i, 2 * (Norm.OWN + 1 + K - 1))
                    for h in range(2):
                        c = 2 * i + h
                        dve.wait_ge(parts_in[h], 16 * K * (i + 1))
                        flat = x[:, bass.ds(c * JC * D, JC * D)]
                        for k in range(K - 1):
                            own(nc.vector.tensor_tensor(flat, flat, part[:, h, k, :], ALU.add))
                        nc.vector.tensor_tensor(flat, flat, part[:, h, K - 1, :], ALU.add).then_inc(parts_used, 1)
                        dve.wait_ge(parts_used, after(c))
                        norm.vector(dve, own, c, lambda k: columns(c, k), dinv[:, line(c * JC, JC)])
                own.leave(NC // 2)
                own.close()

            @block.scalar
            def _(act):
                act.wait_ge(deg_floor, 1)
                nc.scalar.activation(tmp2[:, :], tmp[:, :], ACT.Sqrt).then_inc(deg_root, 1)
                with act.Fori(0, NC // 2) as i:
                    for h in range(2):
                        c = 2 * i + h
                        norm.scalar_std(act, c)
                        act.wait_ge(h_stored[h], 16 * (i + 1))
                        norm.scalar_apply(act, c, lambda k: columns(c, k), lambda k: hout[:, h, k, :], ACT.Relu)

            @block.tensor
            def _(pe):
                pe.wait_ge(hist_summed, 1)
                nc.tensor.matmul(bank[0][:, 0:1], upper[:, :], hist_sum[:, :], start=True,
                                 stop=True).then_inc(hist_offset, 1)

        def edge_layer(name, weights):
            with ExitStack() as ph:
                sums = RunningSums(f"{name}_run", ph)
                ring = Gather(f"{name}_ring", ph, D, sums.summed)
                block = ph.enter_context(nc.Block(name))

                @block.sync
                def _(sp):
                    sums.sync_start(sp)
                    with sp.Fori(0, TURNS) as i:
                        for h in range(2):
                            sums.sync(sp, i, h)

                @block.gpsimd
                def _(pool):
                    ring.pool(pool, h_table)
                    sums.pool_carry(pool, first_end)
                    pool.wait_ge(sums.whole, 16)

                @block.vector
                def _(dve):
                    own = Vector(dve)
                    sums.vector_start(dve, own)
                    with dve.Fori(0, TURNS) as i:
                        own.enter(i, 2 * (RunningSums.OWN + (weights is not None)))
                        for h in range(2):
                            ring.wait_rows(dve, i, h)
                            if weights is not None:
                                here = weights[:, line((2 * i + h) * B, B)]
                                own(nc.vector.tensor_tensor(
                                    ring.rows[:, h, :, :], ring.rows[:, h, :, :],
                                    here.unsqueeze(2).broadcast_to([P, B, D]), ALU.mult))
                            sums.vector(dve, own, i, h, lambda b: ring.rows[:, h, b, :])
                    own.leave(TURNS)
                    sums.vector_carry(dve)
                    own.close()

                @block.scalar
                def _(act):
                    act.sem_inc(ring.staged, 2)
                    with act.Fori(0, TURNS) as i:
                        for h in range(2):
                            ring.scalar_stage(act, src_idx, 2 * i + h, h)
                        if weights is None:
                            act.dma_start(adst_steps[:, line(i * 2 * B, 2 * B), :],
                                          zeros[:, 0:2 * B * RH].rearrange("p (t c) -> p t c", c=RH)
                                          ).then_inc(zeros_out, 16)
                    if weights is None:
                        act.wait_ge(zeros_out, 16 * (TURNS + 1))

                @block.tensor
                def _(pe):
                    sums.tensor_carry(pe, from_before, sums.sums[:, 1, B - 1, :])
                return sums

        layer1 = edge_layer("layer1", None)

        hn_scope = ExitStack()
        hn = sb("hn", [P, J, D], f32, hn_scope)

        def normed(c, k):
            return hn[:, line(c * JC + k, 1), :].rearrange("p a d -> p (a d)")

        with ExitStack() as ph:
            nodes = NodeSums("layer1_nodes", ph, node_row)
            h_stored = [sem(f"h2_stored{h}") for h in range(2)]
            norm = Norm("norm2", ph)
            block = ph.enter_context(nc.Block("nodes2"))

            @block.sync
            def _(sp):
                with sp.Fori(0, NC // 2) as i:
                    for h in range(2):
                        c = 2 * i + h
                        sp.wait_ge(norm.out_ready, c + 1)
                        sp.dma_start(h_columns[:, line(c * JC, JC), :], hn[:, line(c * JC, JC), :]
                                     ).then_inc(h_stored[h], 16)
                for h in range(2):
                    sp.wait_ge(h_stored[h], 16 * (NC // 2))

            @block.gpsimd
            def _(pool):
                nodes.pool(pool, layer1.whole)

            @block.vector
            def _(dve):
                own = Vector(dve)
                dve.sem_inc(nodes.used, 2)
                with dve.Fori(0, NC // 2) as i:
                    own.enter(i, 2 * (1 + Norm.OWN))
                    for h in range(2):
                        c = 2 * i + h
                        nodes.wait_rows(dve, i, h)
                        own(nc.vector.tensor_tensor(
                            nodes.rows[:, h, :, :], nodes.rows[:, h, :, :],
                            dinv[:, line(c * JC, JC)].unsqueeze(2).broadcast_to([P, JC, D]), ALU.mult))
                        nc.vector.tensor_tensor(chunk(c), chunk(c), nodes.rows[:, h, :, :],
                                                ALU.add).then_inc(nodes.used, 1)
                        dve.wait_ge(nodes.used, after(c))
                        norm.vector(dve, own, c, lambda k: columns(c, k))
                own.leave(NC // 2)
                own.close()

            @block.scalar
            def _(act):
                act.sem_inc(nodes.staged, 2)
                with act.Fori(0, NC // 2) as i:
                    for h in range(2):
                        c = 2 * i + h
                        nodes.scalar_stage(act, c, h)
                        norm.scalar_std(act, c)
                        norm.scalar_apply(act, c, lambda k: columns(c, k), lambda k: normed(c, k), ACT.Relu)

        layer2 = edge_layer("layer2", ew_prob)

        with ExitStack() as ph:
            nodes = NodeSums("layer2_nodes", ph, node_row)
            square = sb("square", [P, JC, D], f32, ph)
            sumsq = sb("sumsq", [P, JC], f32, ph)
            length = sb("length", [P, JC], f32, ph)
            inverse = sb("inverse", [P, JC], f32, ph)
            turned = sb("turned", [P, 2, 2 * P], f32, ph)
            hn_here = sb("hn_here", [P, JC, D], f32, ph)
            comb = sb("comb", [P, JC, D], f32, ph)
            hrel = square
            hrel_turned = sb("hrel_turned", [P, 2, P], f32, ph)
            rel_rows = sb("rel_rows", [P, 2, JC, R, XW], f32, ph)
            adst_rows = sb("adst_rows", [P, 2, JC, RH], f32, ph)
            start_stage = sb("start_stage", [P, 2, JC], i32, ph)
            adst_first = sb("adst_first", [P, RH], f32, ph)
            agg_scaled = sem("agg_scaled")
            hn_placed = sem("hn_placed")
            sumsq_ready = sem("sumsq_ready")
            length_ready = sem("length_ready")
            nodes_turned = sem("nodes_turned")
            turned_copied = sem("turned_copied")
            combined = sem("combined")
            comb_copied = sem("comb_copied")
            h_turned = sem("h_turned")
            h_turned_copied = sem("h_turned_copied")
            projected = sem("projected")
            rel_copied = sem("rel_copied")
            scores_copied = sem("scores_copied")
            start_staged = sem("start_staged")
            rel_stored = [sem(f"rel_stored{h}") for h in range(2)]
            adst_stored = [sem(f"adst_stored{h}") for h in range(2)]
            spread = [sem(f"spread{h}") for h in range(2)]
            spread_landed = sem("spread_landed")
            first_got = sem("first_got")
            first_put = sem("first_put")
            comb_norm = Norm("norm_comb", ph)
            norm = Norm("norm3", ph)
            block = ph.enter_context(nc.Block("nodes3"))

            def spare_bank(i, width):
                return row_bank[:, i * 512:i * 512 + width]

            def comb_bank(slot):
                return spare_bank(0, D) if slot else bank[2][:, 0:D]

            def rel_bank(slot):
                return spare_bank(1, R * D) if slot else bank[3][:, 0:R * D]

            def score_bank(slot):
                return spare_bank(2, 2 * RH) if slot else bank[4][:, 0:2 * RH]

            @block.sync
            def _(sp):
                for h in range(2):
                    sp.sem_inc(rel_stored[h], 16)
                    sp.sem_inc(adst_stored[h], 16)
                with sp.Fori(0, NC // 2) as i:
                    for h in range(2):
                        c = 2 * i + h
                        sp.wait_ge(rel_copied, after((c + 1) * JC - 1))
                        sp.wait_ge(scores_copied, after((c + 1) * JC - 1))
                        sp.dma_start(rel_columns[:, line(c * JC, JC), :, :].rearrange("p j r d -> p (j r d)"),
                                     rel_rows[:, h, :, :, :].rearrange("p j r d -> p (j r d)")
                                     ).then_inc(rel_stored[h], 16)
                        sp.dma_start(adst_columns[:, line(c * JC, JC), :], adst_rows[:, h, :, :]
                                     ).then_inc(adst_stored[h], 16)
                for h in range(2):
                    sp.wait_ge(rel_stored[h], 16 * (NC // 2 + 1))
                sp.wait_ge(first_got, 16)
                for h in range(2):
                    sp.wait_ge(spread[h], 16 * JC * (NC // 2))
                sp.dma_start(adst_steps[:, 0, :], adst_first[:, :]).then_inc(first_put, 16)
                sp.wait_ge(first_put, 16)

            @block.gpsimd
            def _(pool):
                pool.sem_inc(spread_landed, 2)

                def gather_sums(c, h):
                    pool.wait_ge(nodes.staged, after(c))
                    pool.wait_ge(nodes.used, after(c - 2))
                    pool.wait_ge(layer2.whole, 16)
                    pool.sem_inc(passed, 1)
                    for k in range(JC):
                        nc.gpsimd.indirect_dma_start(
                            nodes.rows[:, h, k, :], None, running,
                            bass.IndirectOffsetOnAxis(ap=nodes.stage[:, h, k:k + 1], axis=0)
                            ).then_inc(nodes.got[h], 16)

                def spread_scores(c, h):
                    pool.wait_ge(start_staged, after(c))
                    pool.wait_ge(scores_copied, after((c + 1) * JC - 1))
                    pool.sem_inc(passed, 1)
                    for k in range(JC):
                        nc.gpsimd.indirect_dma_start(
                            adst_edges, bass.IndirectOffsetOnAxis(ap=start_stage[:, h, k:k + 1], axis=0),
                            adst_rows[:, h, k, :], None).then_inc(spread[h], 16)

                def await_spread(i, h):
                    pool.wait_ge(spread[h], 16 * JC * (i + 1))
                    pool.sem_inc(spread_landed, 1)

                for h in range(2):
                    gather_sums(h, h)
                with pool.Fori(0, NC // 2 - 1) as i:
                    for h in range(2):
                        c = 2 * i + h
                        gather_sums(c + 2, h)
                        spread_scores(c, h)
                    for h in range(2):
                        await_spread(i, h)
                for h in range(2):
                    spread_scores(NC - 2 + h, h)
                for h in range(2):
                    pool.wait_ge(adst_stored[h], 16 * (NC // 2 + 1))
                nc.gpsimd.indirect_dma_start(
                    adst_first[:, :], None, adst_nodes,
                    bass.IndirectOffsetOnAxis(ap=first_node[:, :], axis=0)).then_inc(first_got, 16)

            @block.vector
            def _(dve):
                own = Vector(dve)
                for s in (nodes.used, comb_copied, scores_copied):
                    dve.sem_inc(s, 2)
                with dve.Fori(0, NC // 2) as i:
                    own.enter(i, 2 * (2 * 3 + 1 + Norm.OWN + 2 + Norm.OWN))
                    for h in range(2):
                        c = 2 * i + h

                        def reciprocal_length(n, of):
                            own(nc.vector.tensor_tensor(square[:, :, :], of, of, ALU.mult))
                            nc.vector.reduce_sum(sumsq[:, :], square[:, :, :], X_AXIS).then_inc(sumsq_ready, 1)
                            dve.wait_ge(length_ready, 2 * c + n + 1)
                            own(nc.vector.tensor_scalar(inverse[:, :], length[:, :], NORM_EPS, None, ALU.add))
                            own(nc.vector.reciprocal(inverse[:, :], inverse[:, :]))
                            return inverse[:, :].unsqueeze(2).broadcast_to([P, JC, D])

                        nodes.wait_rows(dve, i, h)
                        agg = nodes.rows[:, h, :, :]
                        nc.vector.tensor_tensor(agg, agg, reciprocal_length(0, agg),
                                                ALU.mult).then_inc(agg_scaled, 1)
                        for k in range(JC):
                            q = c * JC + k
                            dve.wait_ge(combined, after(q))
                            ins = nc.vector.scalar_tensor_tensor(
                                out=comb[:, k, :], in0=comb_bank((h * JC + k) % 2), scalar=0.5, in1=half_bias[:, :],
                                op0=ALU.mult, op1=ALU.add)
                            ins.then_inc(comb_copied, 1)
                        dve.wait_ge(comb_copied, after((c + 1) * JC - 1))
                        by = reciprocal_length(1, comb[:, :, :])
                        own(nc.vector.tensor_tensor(comb[:, :, :], comb[:, :, :], by, ALU.mult))
                        comb_norm.vector(dve, own, c, lambda k: comb[:, k, :])
                        dve.wait_ge(comb_norm.out_ready, c + 1)
                        own(nc.vector.tensor_tensor(comb[:, :, :], comb[:, :, :],
                                                    gamma[:, :].unsqueeze(1).broadcast_to([P, JC, D]), ALU.mult))
                        own(nc.vector.tensor_tensor(comb[:, :, :], comb[:, :, :],
                                                    beta[:, :].unsqueeze(1).broadcast_to([P, JC, D]), ALU.add))
                        nc.vector.tensor_tensor(chunk(c), chunk(c), comb[:, :, :], ALU.add).then_inc(nodes.used, 1)
                        dve.wait_ge(nodes.used, after(c))
                        norm.vector(dve, own, c, lambda k: columns(c, k))
                        dve.wait_ge(rel_stored[h], 16 * (i + 1))
                        dve.wait_ge(adst_stored[h], 16 * (i + 1))
                        dve.wait_ge(spread_landed, after(c - 2))
                        for k in range(JC):
                            q = c * JC + k
                            dve.wait_ge(projected, after(q))
                            scores = score_bank((h * JC + k) % 2)
                            nc.vector.tensor_copy(rel_rows[:, h, k, :, D:XW],
                                                  scores[:, 0:RH].rearrange("p (r h) -> p r h", r=R))
                            nc.vector.tensor_copy(adst_rows[:, h, k, :], scores[:, RH:2 * RH]
                                                  ).then_inc(scores_copied, 1)
                own.leave(NC // 2)
                own.close()

            @block.scalar
            def _(act):
                for s in (nodes.staged, start_staged, turned_copied, h_turned_copied, rel_copied):
                    act.sem_inc(s, 2)

                def root_of_sumsq(n):
                    act.wait_ge(sumsq_ready, n + 1)
                    nc.scalar.activation(length[:, :], sumsq[:, :], ACT.Sqrt).then_inc(length_ready, 1)

                def chunk_steps(i, h, more):
                    c = 2 * i + h
                    nc.scalar.copy(hn_here[:, :, :], hn[:, line(c * JC, JC), :]).then_inc(hn_placed, 1)
                    root_of_sumsq(2 * c)
                    for k in range(JC):
                        q, slot = c * JC + k, (h * JC + k) % 2
                        act.wait_ge(nodes_turned, after(q))
                        act.wait_ge(combined, after(q - 2))
                        nc.scalar.copy(turned[:, slot, :], bank[slot][:, 0:2 * P]).then_inc(turned_copied, 1)
                    root_of_sumsq(2 * c + 1)
                    comb_norm.scalar_std(act, c)
                    comb_norm.scalar_apply(act, c, lambda k: comb[:, k, :], lambda k: comb[:, k, :],
                                           ACT.Identity)
                    norm.scalar_std(act, c)
                    norm.scalar_apply(act, c, lambda k: columns(c, k), lambda k: hrel[:, k, :], ACT.Relu)
                    if more:
                        nodes.scalar_stage(act, c + 2, h)
                    act.wait_ge(spread_landed, after(c - 2))
                    nc.scalar.copy(start_stage[:, h, :], node_start[:, line(c * JC, JC)]
                                   ).then_inc(start_staged, 1)
                    act.wait_ge(rel_stored[h], 16 * (i + 1))
                    for k in range(JC + 1):
                        q, slot = c * JC + k, (h * JC + k) % 2
                        if k < JC:
                            act.wait_ge(h_turned, after(q))
                            act.wait_ge(projected, after(q - 2))
                            nc.scalar.copy(hrel_turned[:, slot, :], bank[slot][:, 256:256 + P]
                                           ).then_inc(h_turned_copied, 1)
                        if k > 0:
                            act.wait_ge(projected, after(q - 1))
                            nc.scalar.copy(rel_rows[:, h, k - 1, :, 0:D],
                                           rel_bank(1 - slot).rearrange("p (r d) -> p r d", r=R)
                                           ).then_inc(rel_copied, 1)

                for h in range(2):
                    nodes.scalar_stage(act, h, h)
                with act.Fori(0, NC // 2 - 1) as i:
                    for h in range(2):
                        chunk_steps(i, h, True)
                for h in range(2):
                    chunk_steps(NC // 2 - 1, h, False)

            @block.tensor
            def _(pe):
                for s in (nodes_turned, combined, h_turned, projected):
                    pe.sem_inc(s, 2)
                with pe.Fori(0, NC // 2) as i:
                    for h in range(2):
                        c = 2 * i + h
                        pe.wait_ge(agg_scaled, c + 1)
                        pe.wait_ge(hn_placed, c + 1)
                        for k in range(JC + 1):
                            q, slot = c * JC + k, (h * JC + k) % 2
                            if k < JC:
                                pe.wait_ge(turned_copied, after(q - 2))
                                nc.tensor.transpose(bank[slot][:, 0:P], nodes.rows[:, h, k, :], ident[:, :])
                                nc.tensor.transpose(bank[slot][:, P:2 * P], hn_here[:, k, :],
                                                    ident[:, :]).then_inc(nodes_turned, 1)
                            if k > 0:
                                pe.wait_ge(turned_copied, after(q - 1))
                                pe.wait_ge(comb_copied, after(q - 3))
                                nc.tensor.matmul(comb_bank(1 - slot), turned[:, 1 - slot, 0:P], wnb[:, :],
                                                 start=True, stop=False)
                                nc.tensor.matmul(comb_bank(1 - slot), turned[:, 1 - slot, P:2 * P], wself[:, :],
                                                 start=False, stop=True).then_inc(combined, 1)
                        pe.wait_ge(norm.out_ready, c + 1)
                        for k in range(JC + 1):
                            q, slot = c * JC + k, (h * JC + k) % 2
                            if k < JC:
                                pe.wait_ge(h_turned_copied, after(q - 2))
                                nc.tensor.transpose(bank[slot][:, 256:256 + P], hrel[:, k, :],
                                                    ident[:, :]).then_inc(h_turned, 1)
                            if k > 0:
                                pe.wait_ge(h_turned_copied, after(q - 1))
                                pe.wait_ge(rel_copied, after(q - 3))
                                pe.wait_ge(scores_copied, after(q - 3))
                                nc.tensor.matmul(rel_bank(1 - slot), hrel_turned[:, 1 - slot, :], w3[:, :],
                                                 start=True, stop=True)
                                nc.tensor.matmul(score_bank(1 - slot), hrel_turned[:, 1 - slot, :], w3_score[:, :],
                                                 start=True, stop=True).then_inc(projected, 1)
        hn_scope.close()

        S = 2 * B
        assert TURNS % 2 == 0
        with ExitStack() as ph:
            score = sb("score", [P, H, T], f32, ph)
            last_lse = sb("last_lse", [P, RH], f32, ph)

            def by_relation(t):
                return t.rearrange("p (r h) s -> p r h s", r=R)

            with ExitStack() as sub:
                scores_taken = sem("scores_taken")
                kept = [sem(f"kept{h}") for h in range(2)]
                ring = Gather("layer3_ring", sub, XW, scores_taken)
                adst_in = sb("adst_in", [P, 2, S, RH], f32, sub)
                fill = sb("fill", [P, RH, S + 1], f32, sub)
                top = sb("top", [P, RH, S + 1], f32, sub)
                total = sb("total", [P, RH, S + 1], f32, sub)
                typed = sb("typed", [P, RH, S], f32, sub)
                adst_own = sb("adst_own", [P, H, S], f32, sub)
                limit = sb("limit", [P, R, S], f32, sub)
                neg = sb("neg3", [P, 2, S], f32, sub)
                power = sb("power", [P, 2, RH, S], f32, sub)
                floor = sb("floor", [P, RH, S], f32, sub)
                log = sb("log", [P, RH, S], f32, sub)
                run_end = sb("run_end", [P, S], f32, sub)
                lse = sb("lse", [P, 2, S, RH], f32, sub)
                adst_loaded = [sem(f"adst_loaded{g}") for g in range(2)]
                adst_used = sem("adst_used")
                powers_set = sem("powers_set")
                powers_made = sem("powers_made")
                floor_set = sem("floor_set")
                log_made = sem("log_made")
                lse_made = sem("lse_made")
                lse_stored = [sem(f"lse_stored{g}") for g in range(2)]
                block = sub.enter_context(nc.Block("layer3_scores"))

                @block.sync
                def _(sp):
                    for h in range(2):
                        sp.sem_inc(kept[h], 16)
                        sp.sem_inc(lse_stored[h], 16)

                    def load_adst(i, g):
                        sp.wait_ge(adst_used, after(i - 2))
                        sp.dma_start(adst_in[:, g, :, :], adst_steps[:, line(i * S, S), :]
                                     ).then_inc(adst_loaded[g], 16)

                    def keep(i):
                        for h in range(2):
                            sp.wait_ge(ring.got[h], 16 * B * (i + 1))
                            sp.dma_start(rel_steps[:, line((2 * i + h) * B, B), :], ring.rows[:, h, :, :]
                                         ).then_inc(kept[h], 16)

                    def store_lse(i, g):
                        sp.wait_ge(lse_made, after(i))
                        sp.dma_start(lse_steps[:, line(i * S, S), :], lse[:, g, :, :]).then_inc(lse_stored[g], 16)

                    load_adst(0, 0)
                    load_adst(1, 1)
                    keep(0)
                    with sp.Fori(0, TURNS // 2 - 1) as ii:
                        for g in range(2):
                            keep(2 * ii + g + 1)
                            store_lse(2 * ii + g, g)
                            load_adst(2 * ii + g + 2, g)
                    keep(TURNS - 1)
                    for g in range(2):
                        store_lse(TURNS - 2 + g, g)
                    for h in range(2):
                        sp.wait_ge(kept[h], 16 * (TURNS + 1))
                        sp.wait_ge(lse_stored[h], 16 * (TURNS // 2 + 1))

                @block.gpsimd
                def _(pool):
                    with pool.Fori(0, TURNS) as i:
                        for h in range(2):
                            u = 2 * i + h
                            pool.wait_ge(ring.staged, after(u))
                            pool.wait_ge(scores_taken, after(u - 2))
                            pool.wait_ge(kept[h], 16 * (i + 1))
                            pool.sem_inc(passed, 1)
                            for b in range(B):
                                nc.gpsimd.indirect_dma_start(
                                    ring.rows[:, h, b, :], None, rel_table,
                                    bass.IndirectOffsetOnAxis(ap=ring.stage[:, h, b:b + 1], axis=0)
                                    ).then_inc(ring.got[h], 16)

                @block.scalar
                def _(act):
                    act.sem_inc(ring.staged, 2)
                    act.sem_inc(scores_taken, 2)

                    def take(i, h):
                        ring.wait_rows(act, i, h)
                        nc.scalar.copy(score[:, :, line((2 * i + h) * B, B)],
                                       ring.rows[:, h, :, D:XW].rearrange("p b h -> p h b")
                                       ).then_inc(scores_taken, 1)

                    def exponentials(i):
                        act.wait_ge(powers_set, i + 1)
                        nc.scalar.activation(power[:, :, :, :], power[:, :, :, :], ACT.Exp
                                             ).then_inc(powers_made, 1)

                    def logarithms(i):
                        act.wait_ge(floor_set, i + 1)
                        nc.scalar.activation(log[:, :, :], floor[:, :, :], ACT.Ln).then_inc(log_made, 1)

                    for h in range(2):
                        nc.scalar.copy(ring.stage[:, h, :], rel_idx[:, h * B:(h + 1) * B]).then_inc(ring.staged, 1)
                    with act.Fori(0, TURNS - 1) as i:
                        for h in range(2):
                            take(i, h)
                            act.wait_ge(scores_taken, after(2 * i + h))
                            nc.scalar.copy(ring.stage[:, h, :], rel_idx[:, line((2 * i + 2 + h) * B, B)]
                                           ).then_inc(ring.staged, 1)
                        exponentials(i)
                        logarithms(i)
                    for h in range(2):
                        take(TURNS - 1, h)
                    exponentials(TURNS - 1)
                    logarithms(TURNS - 1)

                @block.vector
                def _(dve):
                    own = Vector(dve)
                    dve.sem_inc(adst_used, 2)
                    dve.sem_inc(lse_made, 2)
                    for t, value in ((fill, 0.0), (total, 0.0), (top, -BIG)):
                        own(nc.vector.memset(t[:, :, 0:1], value))
                    with dve.Fori(0, TURNS // 2) as ii:
                        own.enter(ii, 2 * 14)
                        for g in range(2):
                            i = 2 * ii + g
                            steps = line(i * S, S)
                            types = is_type[:, :, steps].unsqueeze(2).broadcast_to([P, R, H, S])
                            nc.vector.tensor_scalar(limit[:, :, :], is_type[:, :, steps], -0.5, 2 * BIG,
                                                    ALU.add, ALU.mult)
                            nc.vector.tensor_scalar(run_end[:, :], same[:, line(i * S + 1, S)], -1.0, 1.0,
                                                    ALU.mult, ALU.add)
                            nc.vector.tensor_scalar(neg[:, 0, :], same[:, steps], -1.0, BIG, ALU.add, ALU.mult)
                            own(nc.vector.tensor_scalar(neg[:, 1, :], same[:, steps], -1.0, 2 * BIG,
                                                        ALU.add, ALU.mult))
                            dve.wait_ge(adst_loaded[g], 16 * (ii + 1))
                            for k in range(RH):
                                ins = nc.vector.tensor_tensor_scan(
                                    fill[:, k, 1:S + 1], same[:, steps], adst_in[:, g, :, k],
                                    fill[:, k, 0:1], ALU.mult, ALU.add)
                            ins.then_inc(adst_used, 1)
                            dve.wait_ge(adst_used, after(i))
                            nc.vector.tensor_copy(fill[:, :, 0:1], fill[:, :, S:S + 1])
                            own(nc.vector.tensor_tensor(by_relation(typed[:, :, :]),
                                                        by_relation(fill[:, :, 1:S + 1]), types, ALU.mult))
                            own(nc.vector.tensor_reduce(
                                adst_own[:, :, :], typed[:, :, :].rearrange("p (r h) s -> p h s r", r=R),
                                X_AXIS, ALU.add))
                            dve.wait_ge(scores_taken, after(2 * i + 1))
                            here = score[:, :, steps]
                            own(nc.vector.tensor_tensor(here, here, adst_own[:, :, :], ALU.add))
                            own(nc.vector.scalar_tensor_tensor(out=here, in0=here, scalar=SLOPE, in1=here,
                                                               op0=ALU.mult, op1=ALU.max))
                            own(nc.vector.tensor_tensor(
                                by_relation(typed[:, :, :]), here.unsqueeze(1).broadcast_to([P, R, H, S]),
                                limit[:, :, :].unsqueeze(2).broadcast_to([P, R, H, S]), ALU.min))
                            for k in range(RH):
                                ins = nc.vector.tensor_tensor_scan(top[:, k, 1:S + 1], neg[:, 0, :], typed[:, k, :],
                                                                   top[:, k, 0:1], ALU.add, ALU.max)
                            own(ins)
                            nc.vector.tensor_tensor(power[:, 1, :, :], typed[:, :, :], top[:, :, 1:S + 1],
                                                    ALU.subtract)
                            own(nc.vector.tensor_tensor(power[:, 0, :, :], top[:, :, 0:S], top[:, :, 1:S + 1],
                                                        ALU.subtract))
                            nc.vector.tensor_tensor(
                                power[:, 0, :, :], power[:, 0, :, :],
                                neg[:, 1, :].unsqueeze(1).broadcast_to([P, RH, S]), ALU.add).then_inc(powers_set, 1)
                            dve.wait_ge(powers_made, i + 1)
                            own(nc.vector.tensor_tensor(by_relation(power[:, 1, :, :]),
                                                        by_relation(power[:, 1, :, :]), types, ALU.mult))
                            for k in range(RH):
                                ins = nc.vector.tensor_tensor_scan(total[:, k, 1:S + 1], power[:, 0, k, :],
                                                                   power[:, 1, k, :], total[:, k, 0:1],
                                                                   ALU.mult, ALU.add)
                            own(ins)
                            nc.vector.tensor_scalar(floor[:, :, :], total[:, :, 1:S + 1], 0.5, None,
                                                    ALU.max).then_inc(floor_set, 1)
                            own(nc.vector.tensor_copy(total[:, :, 0:1], total[:, :, S:S + 1]))
                            dve.wait_ge(log_made, i + 1)
                            dve.wait_ge(lse_stored[g], 16 * (ii + 1))
                            own(nc.vector.tensor_tensor(log[:, :, :], log[:, :, :], top[:, :, 1:S + 1], ALU.add))
                            nc.vector.tensor_tensor(
                                lse[:, g, :, :].rearrange("p s c -> p c s"), log[:, :, :],
                                run_end[:, :].unsqueeze(1).broadcast_to([P, RH, S]), ALU.mult
                                ).then_inc(lse_made, 1)
                            own(nc.vector.tensor_copy(top[:, :, 0:1], top[:, :, S:S + 1]))
                            dve.wait_ge(lse_made, after(i))
                            own(nc.vector.tensor_copy(last_lse[:, :], lse[:, g, S - 1, :]))
                    own.leave(TURNS // 2)
                    own.close()

            with ExitStack() as sub:
                diag = sb("diag3", [P, 2, RH, P], f32, sub)
                parts = sb("parts", [P, 2, RH, P], f32, sub)
                bias = sb("bias3", [P, 2, 2, P], f32, sub)
                first_lse = sb("first_lse", [P, RH], f32, sub)
                most = sb("most", [P, 3, RH], f32, sub)
                sums3 = sb("sums3", [P, 3, RH], f32, sub)
                joined = sb("joined", [P, 2, RH], f32, sub)
                first_read = sem("first_read")
                diag_set = sem("diag3_set")
                spread_made = sem("spread3_made")
                parts_set = sem("parts_set")
                parts_exp = sem("parts_exp")
                sum_set = sem("sum3_set")
                sum_log = sem("sum3_log")
                joins_made = sem("joins_made")
                first_patched = sem("first_patched")
                last_patched = sem("last_patched")
                block = sub.enter_context(nc.Block("layer3_join"))
                QUARTER = RH // 4

                @block.gpsimd
                def _(pool):
                    nc.gpsimd.indirect_dma_start(first_lse[:, :], None, lse_edges,
                                                 bass.IndirectOffsetOnAxis(ap=first_end[:, :], axis=0)
                                                 ).then_inc(first_read, 16)
                    pool.wait_ge(joins_made, 2)
                    nc.gpsimd.indirect_dma_start(lse_edges, bass.IndirectOffsetOnAxis(ap=first_end[:, :], axis=0),
                                                 joined[:, 0, :], None).then_inc(first_patched, 16)

                @block.sync
                def _(sp):
                    sp.wait_ge(first_patched, 16)
                    sp.dma_start(lse_steps[:, T - 1, :], joined[:, 1, :]).then_inc(last_patched, 16)
                    sp.wait_ge(last_patched, 16)

                @block.vector
                def _(dve):
                    own = Vector(dve)
                    dve.wait_ge(first_read, 16)
                    for side, ends in enumerate((last_lse, first_lse)):
                        ins = nc.vector.tensor_tensor(
                            diag[:, side, :, :], ident[:, :].unsqueeze(1).broadcast_to([P, RH, P]),
                            ends[:, :].unsqueeze(2).broadcast_to([P, RH, P]), ALU.mult)
                    ins.then_inc(diag_set, 1)
                    nc.vector.tensor_copy(bias[:, 0, 0, :], bias_before[:, :])
                    nc.vector.tensor_scalar(bias[:, 0, 1, :], bias_after[:, :], apart[:, :], None, ALU.add)
                    nc.vector.tensor_scalar(bias[:, 1, 0, :], bias_before[:, :], apart[:, :], None, ALU.add)
                    own(nc.vector.tensor_copy(bias[:, 1, 1, :], bias_after[:, :]))
                    for end, own_part in enumerate((first_lse, last_lse)):
                        for side in range(2):
                            dve.wait_ge(spread_made, 2 * end + side + 1)
                            for q in range(4):
                                at = slice(q * QUARTER, (q + 1) * QUARTER)
                                ins = nc.vector.tensor_tensor(
                                    parts[:, side, at, :], bank[q][:, :].rearrange("p (c q) -> p c q", q=P),
                                    bias[:, end, side, :].unsqueeze(1).broadcast_to([P, QUARTER, P]), ALU.add)
                            ins.then_inc(parts_set, 1)
                            dve.wait_ge(parts_set, 2 * end + side + 1)
                        own(nc.vector.tensor_reduce(most[:, 0:2, :], parts[:, :, :, :], X_AXIS, ALU.max))
                        own(nc.vector.tensor_tensor(most[:, 2, :], most[:, 0, :], most[:, 1, :], ALU.max))
                        own(nc.vector.tensor_tensor(most[:, 2, :], most[:, 2, :], own_part[:, :], ALU.max))
                        nc.vector.tensor_tensor(sums3[:, 2, :], own_part[:, :], most[:, 2, :], ALU.subtract)
                        for side in range(2):
                            ins = nc.vector.tensor_tensor(
                                parts[:, side, :, :], parts[:, side, :, :],
                                most[:, 2, :].unsqueeze(2).broadcast_to([P, RH, P]), ALU.subtract)
                        ins.then_inc(sum_set, 1)
                        dve.wait_ge(parts_exp, end + 1)
                        own(nc.vector.reduce_sum(sums3[:, 0:2, :], parts[:, :, :, :], X_AXIS))
                        own(nc.vector.tensor_tensor(sums3[:, 0, :], sums3[:, 0, :], sums3[:, 1, :], ALU.add))
                        nc.vector.tensor_tensor(sums3[:, 0, :], sums3[:, 0, :], sums3[:, 2, :],
                                                ALU.add).then_inc(sum_set, 1)
                        dve.wait_ge(sum_log, end + 1)
                        nc.vector.tensor_tensor(joined[:, end, :], sums3[:, 1, :], most[:, 2, :],
                                                ALU.add).then_inc(joins_made, 1)
                        dve.wait_ge(joins_made, end + 1)
                    own.close()

                @block.scalar
                def _(act):
                    for end in range(2):
                        act.wait_ge(sum_set, 2 * end + 1)
                        nc.scalar.activation(parts[:, :, :, :], parts[:, :, :, :], ACT.Exp)
                        nc.scalar.activation(sums3[:, 2, :], sums3[:, 2, :], ACT.Exp).then_inc(parts_exp, 1)
                        act.wait_ge(sum_set, 2 * end + 2)
                        nc.scalar.activation(sums3[:, 1, :], sums3[:, 0, :], ACT.Ln).then_inc(sum_log, 1)

                @block.tensor
                def _(pe):
                    pe.wait_ge(diag_set, 1)
                    for turn in range(4):
                        if turn:
                            pe.wait_ge(parts_set, turn)
                        for q in range(4):
                            ins = nc.tensor.matmul(
                                bank[q][:, :], ones[:, :],
                                diag[:, turn % 2, q * QUARTER:(q + 1) * QUARTER, :].rearrange("p c q -> p (c q)"),
                                start=True, stop=True)
                        ins.then_inc(spread_made, 1)

            with ExitStack() as sub:
                sums = RunningSums("layer3_run", sub)
                rel_rows = sb("rel_rows3", [P, 2, B, XW], f32, sub)
                message = sb("message", [P, 2, B, D], f32, sub)
                lse_in = sb("lse_in", [P, 2, S, RH], f32, sub)
                goes_on = sb("goes_on", [P, 2, S], f32, sub)
                holds = sb("holds", [P, 2, RH, S + 1], f32, sub)
                end_lse = sb("end_lse", [P, 2, RH, S + 1], f32, sub)
                held = sb("held", [P, RH, S + 1], f32, sub)
                typed = sb("typed2", [P, RH, S], f32, sub)
                own_lse = sb("own_lse", [P, H, S], f32, sub)
                weight = sb("weight", [P, 2, H, S], f32, sub)
                rel_in = [sem(f"rel_in{h}") for h in range(2)]
                lse_loaded = [sem(f"lse_loaded{g}") for g in range(2)]
                lse_used = sem("lse_used")
                prepared = sem("prepared")
                shifts_made = sem("shifts_made")
                weights_made = sem("weights_made")
                messages_made = sem("messages_made")
                block = sub.enter_context(nc.Block("layer3_sums"))

                @block.sync
                def _(sp):
                    sums.sync_start(sp)

                    def load_rows(i, h):
                        sp.wait_ge(messages_made, after(2 * i + h - 2))
                        sp.sem_inc(passed, 1)
                        sp.dma_start(rel_rows[:, h, :, :],
                                     rel_steps[:, line(T - (2 * i + h + 1) * B, B), :]).then_inc(rel_in[h], 16)

                    def load_lse(i, g):
                        sp.wait_ge(lse_used, after(i - 2))
                        sp.sem_inc(passed, 1)
                        sp.dma_start(lse_in[:, g, :, :], lse_steps[:, line(T - (i + 1) * S, S), :]
                                     ).then_inc(lse_loaded[g], 16)

                    def store(i):
                        for h in range(2):
                            sp.wait_ge(sums.summed, after(2 * i + h))
                            sp.sem_inc(passed, 1)
                            sp.dma_start(running_steps[:, line(T - (2 * i + h + 1) * B, B), :], sums.sums[:, h, :, :]
                                         ).then_inc(sums.stored[h], 16)

                    for g in range(2):
                        load_lse(g, g)
                    for h in range(2):
                        load_rows(0, h)
                    with sp.Fori(0, TURNS // 2 - 1) as ii:
                        for g in range(2):
                            i = 2 * ii + g
                            load_lse(i + 2, g)
                            for h in range(2):
                                load_rows(i + 1, h)
                            store(i)
                    for h in range(2):
                        load_rows(TURNS - 1, h)
                    for i in (TURNS - 2, TURNS - 1):
                        store(i)

                @block.gpsimd
                def _(pool):
                    pool.sem_inc(messages_made, 2)

                    def messages(i, g):
                        pool.wait_ge(weights_made, i + 1)
                        for h in range(2):
                            pool.wait_ge(rel_in[h], 16 * (i + 1))
                            pool.wait_ge(sums.summed, after(2 * i + h - 2))
                            upper_half = weight[:, g, :, (1 - h) * B:(2 - h) * B].rearrange("p h b -> p b h")
                            nc.gpsimd.tensor_tensor(
                                message[:, h, :, :].rearrange("p b (h d) -> p b h d", d=HD),
                                rel_rows[:, h, :, 0:D].rearrange("p b (h d) -> p b h d", d=HD),
                                upper_half.unsqueeze(3).broadcast_to([P, B, H, HD]), ALU.mult
                                ).then_inc(messages_made, 1)

                    with pool.Fori(0, TURNS // 2) as ii:
                        for g in range(2):
                            messages(2 * ii + g, g)
                    sums.pool_carry(pool, last_start)
                    pool.wait_ge(sums.whole, 16)

                @block.scalar
                def _(act):
                    act.sem_inc(lse_used, 2)

                    def exponentials(i, g):
                        act.wait_ge(shifts_made, i + 1)
                        nc.scalar.activation(weight[:, g, :, :], own_lse[:, :, :], ACT.Exp
                                             ).then_inc(weights_made, 1)

                    def prepare(i, ii, g):
                        act.wait_ge(lse_loaded[g], 16 * (ii + 1))
                        nc.scalar.copy(end_lse[:, g, :, 0:S], lse_in[:, g, :, :].rearrange("p s c -> p c s")
                                       ).then_inc(lse_used, 1)
                        nc.scalar.copy(holds[:, g, :, 0:S],
                                       same[:, line(T - (i + 1) * S + 1, S)].unsqueeze(1).broadcast_to([P, RH, S])
                                       ).then_inc(prepared, 1)

                    for g in range(2):
                        prepare(g, 0, g)
                    for g in range(2):
                        exponentials(g, g)
                        prepare(g + 2, 1, g)
                    with act.Fori(1, TURNS // 2 - 1) as ii:
                        for g in range(2):
                            i = 2 * ii + g
                            act.wait_ge(messages_made, after(2 * i - 3))
                            exponentials(i, g)
                            prepare(i + 2, ii + 1, g)
                    for g in range(2):
                        act.wait_ge(messages_made, after(2 * (TURNS - 2 + g) - 3))
                        exponentials(TURNS - 2 + g, g)

                @block.vector
                def _(dve):
                    own = Vector(dve)
                    sums.vector_start(dve, own)
                    nc.vector.memset(holds[:, :, :, S:S + 1], 0.0)
                    own(nc.vector.memset(end_lse[:, 0, :, S:S + 1], 0.0))

                    def backwards(t):
                        return t.rearrange("p c s -> p (c s)")[:, ::-1]

                    def weights(i, ii, g, after_first=True):
                        start = T - (i + 1) * S
                        steps, ahead = line(start, S), same[:, line(start + 1, S)]
                        if after_first:
                            dve.wait_ge(sums.summed, after(2 * i - 3))
                        nc.vector.tensor_copy(goes_on[:, g, :], ahead)
                        dve.wait_ge(prepared, i + 1)
                        own(nc.vector.tensor_tensor_scan(
                            backwards(held[:, :, :]), backwards(holds[:, g, :, :]),
                            backwards(end_lse[:, g, :, :]), 0.0, ALU.mult, ALU.add))
                        nc.vector.tensor_copy(end_lse[:, 1 - g, :, S:S + 1], held[:, :, 0:1])
                        own(nc.vector.tensor_tensor(
                            by_relation(typed[:, :, :]), by_relation(held[:, :, 0:S]),
                            is_type[:, :, steps].unsqueeze(2).broadcast_to([P, R, H, S]), ALU.mult))
                        if after_first:
                            dve.wait_ge(weights_made, i)
                        own(nc.vector.tensor_reduce(
                            own_lse[:, :, :], typed[:, :, :].rearrange("p (r h) s -> p h s r", r=R),
                            X_AXIS, ALU.add))
                        nc.vector.tensor_tensor(own_lse[:, :, :], score[:, :, steps], own_lse[:, :, :],
                                                ALU.subtract).then_inc(shifts_made, 1)

                    def run(i, g, h):
                        u = 2 * i + h
                        at = (1 - h) * B
                        dve.wait_ge(messages_made, after(u))
                        dve.wait_ge(sums.stored[h], 16 * (i + 1))
                        dve.wait_ge(sums.summed, after(u - 1))
                        for b in reversed(range(B)):
                            later = sums.sums[:, h, b + 1, :] if b < B - 1 else sums.sums[:, 1 - h, 0, :]
                            ins = nc.vector.scalar_tensor_tensor(
                                out=sums.sums[:, h, b, :], in0=later, scalar=goes_on[:, g, at + b:at + b + 1],
                                in1=message[:, h, b, :], op0=ALU.mult, op1=ALU.add)
                            if b:
                                own(ins)
                        ins.then_inc(sums.summed, 1)

                    weights(0, 0, 0, after_first=False)
                    with dve.Fori(0, TURNS // 2 - 1) as ii:
                        own.enter(ii, 2 * (3 + 2 * (B - 1)))
                        for g in range(2):
                            i = 2 * ii + g
                            weights(i + 1, ii + g, 1 - g)
                            for h in range(2):
                                run(i, g, h)
                    own.leave(TURNS // 2 - 1)
                    weights(TURNS - 1, TURNS // 2 - 1, 1)
                    for g in range(2):
                        for h in range(2):
                            run(TURNS - 2 + g, g, h)
                    sums.vector_carry(dve)
                    own.close()

                @block.tensor
                def _(pe):
                    sums.tensor_carry(pe, from_after, sums.sums[:, 1, 0, :])
                layer3 = sums

        with ExitStack() as ph:
            nodes = NodeSums("layer3_nodes", ph, node_first)
            stored = sem("out_stored")
            block = ph.enter_context(nc.Block("nodes4"))

            @block.sync
            def _(sp):
                sp.wait_ge(nodes.used, after(NC - 1))
                whole = N // J
                stores = 0
                for a, b in ((0, whole // 16 * 16), (whole // 16 * 16, whole)):
                    if b > a:
                        sp.dma_start(out[a * J:b * J, :].rearrange("(p j) d -> p (j d)", j=J),
                                     x[a:b, :]).then_inc(stored, 16)
                        stores += 1
                rest = N - whole * J
                if rest:
                    sp.dma_start(out[whole * J:N, :].rearrange("(a j) d -> a (j d)", a=1),
                                 x[whole:whole + 1, 0:rest * D]).then_inc(stored, 16)
                    stores += 1
                sp.wait_ge(stored, 16 * stores)

            @block.gpsimd
            def _(pool):
                nodes.pool(pool, layer3.whole)

            @block.vector
            def _(dve):
                own = Vector(dve)
                dve.sem_inc(nodes.used, 2)
                with dve.Fori(0, NC // 2) as i:
                    own.enter(i, 0)
                    for h in range(2):
                        c = 2 * i + h
                        nodes.wait_rows(dve, i, h)
                        nc.vector.tensor_tensor(chunk(c), chunk(c), nodes.rows[:, h, :, :],
                                                ALU.add).then_inc(nodes.used, 1)
                own.leave(NC // 2)
                own.close()

            @block.scalar
            def _(act):
                act.sem_inc(nodes.staged, 2)
                with act.Fori(0, NC // 2) as i:
                    for h in range(2):
                        nodes.scalar_stage(act, 2 * i + h, h)


_INS = ["x", "src", "dst", "edge_type", "edge_weight", "tile_src", "tile_src_cols", "edge_attr", "w0", "b0",
        "w_self", "w_nb", "b_self", "b_nb", "gamma", "beta", "w3", "attn"]


def lay_out(x, src, dst, edge_attr_256, edge_type_4, edge_weight, L0_gnn_W, L0_gnn_b, L2_gnn_W_self,
            L2_gnn_b_self, L2_gnn_W_nb, L2_gnn_b_nb, L2_gnn_gamma, L2_gnn_beta, L3_gnn_W, L3_gnn_attn):
    import numpy as np

    x, src, dst = np.asarray(x), np.asarray(src), np.asarray(dst)
    n, e = x.shape[0], src.shape[0]
    j, t = node_columns(n), steps_per_partition(e)
    groups = 2 * (e // (2 * G * P))
    tiles = (groups + 1) * G

    def padded(a, size, value):
        return np.concatenate([a, np.full((size - a.shape[0],) + a.shape[1:], value, a.dtype)])

    def by_partition(a, value):
        return np.ascontiguousarray(padded(np.asarray(a), P * t, value).reshape(P, t))

    def on_all(a):
        return np.ascontiguousarray(np.broadcast_to(np.asarray(a).reshape(1, -1), (P, a.size)))

    pad_node = P * j - 1
    order = src[:groups * G * P].reshape(groups, P, G).transpose(0, 2, 1).reshape(-1)
    tile_src = padded(np.concatenate([order, src[groups * G * P:]]), tiles * P, pad_node)
    attn = np.asarray(L3_gnn_attn).reshape(R, H, 2, HD).transpose(2, 0, 1, 3)
    w3 = np.asarray(L3_gnn_W).transpose(1, 0, 2).reshape(D, R * D)
    arrays = [
        padded(x, P * j, 0).reshape(P, j * D), by_partition(src, pad_node), by_partition(dst, pad_node),
        by_partition(edge_type_4, 0), by_partition(edge_weight, 0), tile_src,
        np.ascontiguousarray(tile_src.reshape(tiles, P).T), np.asarray(edge_attr_256),
        np.asarray(L0_gnn_W), on_all(L0_gnn_b), np.asarray(L2_gnn_W_self), np.asarray(L2_gnn_W_nb),
        on_all(L2_gnn_b_self), on_all(L2_gnn_b_nb), on_all(L2_gnn_gamma), on_all(L2_gnn_beta),
        np.ascontiguousarray(w3), on_all(np.ascontiguousarray(attn)),
    ]
    return n, [np.ascontiguousarray(a) for a in arrays]


def kernel(**inputs):
    from concourse import bacc
    from concourse.bass_utils import run_bass_kernel_spmd

    n, arrays = lay_out(**inputs)
    nc = bacc.Bacc("TRN2", target_bir_lowering=False, num_devices=1)
    given = {f"in_{name}": a for name, a in zip(_INS, arrays)}
    args = [nc.dram_tensor(name, a.shape, mybir.dt.from_np(a.dtype), kind="ExternalInput").ap()
            for name, a in given.items()]
    args.append(nc.dram_tensor("out_x", (n, D), mybir.dt.float32, kind="ExternalOutput").ap())
    build_gnn(nc, *args)
    return run_bass_kernel_spmd(nc, [given], core_ids=[0]).results[0]["out_x"]
```
